# Optimizing a Trainium2 kernel written in Bass

```python
import numpy as np
import jax
import jax.numpy as jnp

def _softmax(x, axis=-1):
    return jax.nn.softmax(x, axis=axis)

def _gelu(x):
    return jax.nn.gelu(x, approximate=True)

def _silu(x):
    return jax.nn.silu(x)

def _sigmoid(x):
    return jax.nn.sigmoid(x)

def _layernorm(x, axis=-1, eps=1e-05):
    m = jnp.mean(x, axis=axis, keepdims=True)
    v = jnp.var(x, axis=axis, keepdims=True)
    return (x - m) / jnp.sqrt(v + eps)

def _scatter_add(tgt, idx, src, axis=0):
    return tgt.at[idx].add(src)

def _segment_sum(src, seg, n):
    return jax.ops.segment_sum(src, seg, n)
kernel_name = 'mk_macaron_d1_jaxref_r8_7b8864'

def setup_inputs(seed: int=0):
    np.random.seed(seed)
    _w = jnp.asarray

    def _L0_attn_setup():
        import jax, jax.numpy as jnp
        import numpy as np
        B, S, E, H, G = (2, 256, 256, 16, 4)
        D = E // H
        key = jax.random.key(seed)
        ks = jax.random.split(key, 7)
        scale = 1.0 / np.sqrt(E)
        x = jax.random.normal(ks[0], (B, S, E), dtype=jnp.float32)
        Wq = jax.random.normal(ks[1], (H, E, D), dtype=jnp.float32) * scale
        bq = jax.random.normal(ks[2], (H, D), dtype=jnp.float32) * 0.02
        Wk = jax.random.normal(ks[3], (G, E, D), dtype=jnp.float32) * scale
        bk = jax.random.normal(ks[4], (G, D), dtype=jnp.float32) * 0.02
        Wv = jax.random.normal(ks[5], (G, E, D), dtype=jnp.float32) * scale
        bv = jax.random.normal(ks[6], (G, D), dtype=jnp.float32) * 0.02
        return {'x': x, 'Wq': Wq, 'bq': bq, 'Wk': Wk, 'bk': bk, 'Wv': Wv, 'bv': bv}
    _L0_attn_in = _L0_attn_setup()

    def _L0_ffn_setup():
        import jax, jax.numpy as jnp
        import numpy as np
        H, I, E = (256, 512, 8)
        B, S = (2, 256)
        key = jax.random.key(seed)
        ks = jax.random.split(key, 5)
        scale = 0.02
        return {'hidden_states': jax.random.normal(ks[0], (B, S, H), dtype=jnp.float32), 'router_w': jax.random.normal(ks[1], (H, E), dtype=jnp.float32) * scale, 'gate_w': jax.random.normal(ks[2], (E, H, I), dtype=jnp.float32) * scale, 'up_w': jax.random.normal(ks[3], (E, H, I), dtype=jnp.float32) * scale, 'down_w': jax.random.normal(ks[4], (E, I, H), dtype=jnp.float32) * scale}
    _L0_ffn_in = _L0_ffn_setup()
    _d = {'L0_attn_x': _L0_attn_in['x'], 'L0_attn_Wq': _L0_attn_in['Wq'], 'L0_attn_bq': _L0_attn_in['bq'], 'L0_attn_Wk': _L0_attn_in['Wk'], 'L0_attn_bk': _L0_attn_in['bk'], 'L0_attn_Wv': _L0_attn_in['Wv'], 'L0_attn_bv': _L0_attn_in['bv'], 'L0_ffn_router_w': _L0_ffn_in['router_w'], 'L0_ffn_gate_w': _L0_ffn_in['gate_w'], 'L0_ffn_up_w': _L0_ffn_in['up_w'], 'L0_ffn_down_w': _L0_ffn_in['down_w']}
    _x0 = _d['L0_attn_x']
    _d['L0_attn_x'] = jax.random.normal(jax.random.fold_in(jax.random.key(seed), 1), (8, 256, 256), dtype=_x0.dtype)
    del _x0
    return _d

def reference(L0_attn_x, L0_attn_Wq, L0_attn_bq, L0_attn_Wk, L0_attn_bk, L0_attn_Wv, L0_attn_bv, L0_ffn_router_w, L0_ffn_gate_w, L0_ffn_up_w, L0_ffn_down_w):

    def _L0_attn_ref(x, Wq, bq, Wk, bk, Wv, bv):
        import jax, jax.numpy as jnp
        import numpy as np
        B, S, E, H, G = (2, 256, 256, 16, 4)
        D = E // H
        h, e, d = Wq.shape
        g = Wk.shape[0]
        per = h // g
        s = x.shape[1]
        q = jnp.einsum('bse,hed->bhsd', x, Wq) + bq[None, :, None, :]
        kg = jnp.einsum('bse,ged->bgsd', x, Wk) + bk[None, :, None, :]
        vg = jnp.einsum('bse,ged->bgsd', x, Wv) + bv[None, :, None, :]
        k = jnp.repeat(kg, per, axis=1)
        v = jnp.repeat(vg, per, axis=1)
        scores = jnp.einsum('bhqd,bhkd->bhqk', q, k) * (1.0 / np.sqrt(d))
        causal = jnp.triu(jnp.ones((s, s), dtype=bool), k=1)
        scores = jnp.where(causal[None, None, :, :], -jnp.inf, scores)
        attn = jax.nn.softmax(scores, axis=-1)
        out = jnp.einsum('bhqk,bhkd->bhqd', attn, v)
        return out.transpose(0, 2, 1, 3).reshape(x.shape[0], s, h * d)

    def _L0_ffn_ref(hidden_states, router_w, gate_w, up_w, down_w):
        import jax, jax.numpy as jnp
        import numpy as np
        H, I, E = (256, 512, 8)
        B, S = (2, 256)
        hidden_shape = hidden_states.shape
        x = hidden_states.reshape(-1, hidden_shape[-1])
        route = jax.nn.sigmoid(x @ router_w)
        max_ind = jnp.argmax(route, axis=1)
        max_prob = jnp.take_along_axis(route, max_ind[:, None], axis=1)
        out = jnp.zeros_like(x)
        num_experts = gate_w.shape[0]
        for e in range(num_experts):
            mask = (max_ind == e)[:, None]
            h = jax.nn.silu(x @ gate_w[e]) * (x @ up_w[e])
            out = out + jnp.where(mask, h @ down_w[e], 0.0)
        out = out * max_prob
        return out.reshape(hidden_shape)
    x = L0_attn_x
    x = x + 0.5 * _L0_ffn_ref(_layernorm(x, axis=-1), L0_ffn_router_w, L0_ffn_gate_w, L0_ffn_up_w, L0_ffn_down_w)
    x = x + _L0_attn_ref(_layernorm(x, axis=-1), L0_attn_Wq, L0_attn_bq, L0_attn_Wk, L0_attn_bk, L0_attn_Wv, L0_attn_bv)
    x = x + 0.5 * _L0_ffn_ref(_layernorm(x, axis=-1), L0_ffn_router_w, L0_ffn_gate_w, L0_ffn_up_w, L0_ffn_down_w)
    return x

_drawn_inputs = setup_inputs


def setup_inputs(seed=0):
    import zlib

    import numpy as np

    out = dict(_drawn_inputs(seed))
    spreads = {}
    factors = {'L0_attn_bq': 8.0,
     'L0_attn_bk': 8.0,
     'L0_ffn_router_w': 4.376,
     'L0_ffn_gate_w': 4.08,
     'L0_ffn_up_w': 4.045,
     'L0_ffn_down_w': 4.043}
    for name, (base, spread) in spreads.items():
        noise = np.random.default_rng([zlib.crc32(name.encode()), seed]).standard_normal(out[name].shape)
        drawn = base * np.exp(spread * noise) if base else spread * noise
        out[name] = jnp.asarray(drawn.astype(out[name].dtype))
    for name, factor in factors.items():
        out[name] = (out[name] * factor).astype(out[name].dtype)
    return out
```

```python
from contextlib import ExitStack

import concourse.bass as bass
import numpy as np
from concourse import mybir

F32 = mybir.dt.float32
BF16 = mybir.dt.bfloat16
I32 = mybir.dt.int32
ALU = mybir.AluOpType
ACT = mybir.ActivationFunctionType
AX = mybir.AxisListType

P = 128
B, S, H = 8, 256, 256
T = B * S
NT = T // P
C = H // P
TB = S // P
NE, I = 8, 512
IC = I // P
NS = NT + NE - 1
WE = 3 * C * I
NH, NG, D = 16, 4, 16
HG = NH // NG
PAD = 2 * T
EPS = 1e-5
RSQRT_MAGIC = float(0x5F3759DF)
NEG = -1e30
Q_PART = (0, 0, 1, 1, 0, 2)
K_PART = (0, 1, 0, 1, 2, 0)
KROWS = len(Q_PART) * D
XG, OB, QB = 4, 4, 3

CONST = {"ident": P, "c128": NS + 1, "desc": NE, "lower": NE * NE, "jrow": NS, "toks": NT * 2}
CONST_AT = dict(zip(CONST, np.cumsum([0] + list(CONST.values())[:-1]).tolist()))
CONST_N = sum(CONST.values())
CONSTB = {"identb": P, "before": P, "ones": P, "iota": P, "mask": HG * P}
CONSTB_AT = dict(zip(CONSTB, np.cumsum([0] + list(CONSTB.values())[:-1]).tolist()))
CONSTB_N = sum(CONSTB.values())


def constants():
    p = np.arange(P)
    f = np.zeros((P, CONST_N), np.float32)
    b = np.zeros((P, CONSTB_N), np.float32)

    def put(a, at, name, v):
        v = np.asarray(v, np.float32).reshape(-1, np.asarray(v).shape[-1])
        a[:, at[name]:at[name] + v.shape[1]] = v

    put(f, CONST_AT, "ident", np.eye(P))
    put(f, CONST_AT, "c128", np.arange(NS + 1)[None] * P)
    put(f, CONST_AT, "desc", NE - np.arange(NE)[None])
    put(f, CONST_AT, "lower", (np.arange(NE)[None, :] < np.arange(NE)[:, None]).reshape(1, -1))
    put(f, CONST_AT, "jrow", np.arange(NS)[None])
    toks = np.zeros((P, NT, 2))
    toks[:, :, 0] = P * np.arange(NT)[None] - PAD
    toks[:, :, 1] = p[:, None]
    put(f, CONST_AT, "toks", toks.reshape(P, -1))
    put(b, CONSTB_AT, "identb", np.eye(P))
    put(b, CONSTB_AT, "before", p[:, None] < p[None, :])
    put(b, CONSTB_AT, "ones", np.ones((1, P)))
    put(b, CONSTB_AT, "iota", p[None, :])
    put(b, CONSTB_AT, "mask", np.tile(np.where(p[None, :] > p[:, None], NEG, 0.0), (1, HG)))
    return f, b


def macaron(nc, x, wq, bq, wk, bk, wv, bv, router, gate, up, down, constf, constb, out, stop=None):
    with ExitStack() as ctx:
        def sb(name, shape, dt=F32):
            return ctx.enter_context(nc.sbuf_tensor(name, shape, dt))

        def sem(name):
            return ctx.enter_context(nc.semaphore(name))

        def dram(name, shape, dt=F32):
            return nc.dram_tensor(name, shape, dt).ap()

        rows = [dram(f"rows{l}", (T, 2 * H)) for l in range(2)]
        x2d = dram("x2d", (T, H))
        qd = dram("qd", (QB, 3, NH * D, S), BF16)
        kd = dram("kd", (QB, 3, NG * D, S), BF16)
        md = dram("md", (QB, NH, S), BF16)
        ffn_out = [x2d, out]

        W = sb("W", [P, NE * WE])
        xt = sb("xt", [P, NT, H])
        xn = sb("xn", [P, 2, TB, H])
        xnT = sb("xnT", [P, 2, C, S])
        xnr = sb("xnr", [P, TB, H])
        xnrT = sb("xnrT", [P, C, S])
        wr = sb("wr", [P, C, NE])
        wq_s = sb("wq_s", [P, C, NH * D])
        wk_s = sb("wk_s", [P, C, NG * D])
        wv_s = sb("wv_s", [P, C, NG * D])
        bq_s = sb("bq_s", [P, 2])
        bk_s = sb("bk_s", [NG * D, 1])
        bv_s = sb("bv_s", [P, NG * D])
        cf = sb("cf", [P, CONST_N])
        cb = sb("cb", [P, CONSTB_N], BF16)
        bn = sb("bn", [P, NT, 6])
        mv = sb("mv", [P, NT, 2])
        ve = sb("ve", [P, NT])
        hv = sb("hv", [P, NT], I32)
        rs = sb("rs", [P, NT], I32)
        nw = sb("nw", [P, NT])
        lg = sb("lg", [P, NT, NE])
        sg = sb("sg", [P, NT, NE])
        mx = sb("mx", [P, NT])
        eq = sb("eq", [P, NT, NE])
        pm = sb("pm", [P, NT])
        oh = sb("oh", [P, NT, NE], BF16)
        tot = sb("tot", [P, NE])
        tgt = sb("tgt", [P, NE, NT])
        ntl = sb("ntl", [P, NE])
        lw = sb("lw", [P, NE, NE])
        bt = sb("bt", [P, 3, NE])
        rk = sb("rk", [P, NT, NE])
        pos = sb("pos", [P, NT])
        eg = sb("eg", [1, NS, NE])
        ef = sb("ef", [1, 2, NS])
        eoff = sb("eoff", [1, NS], I32)
        gj = sb("gj", [P, NT, NS + 1])
        jt = sb("jt", [P, 2, NT])
        rb = sb("rb", [P, NT], BF16)
        J = sb("J", [P, NT, NS])
        vals = sb("vals", [P, NT, 5])
        mh = sb("mh", [P, NT, 2], BF16)
        mr = sb("mr", [P, NT])
        R1 = sb("R1", [P, NT, P], BF16)
        J5 = sb("J5", [P, NT, 5, NS], BF16)
        sl = sb("sl", [P, 5, NS])
        tf = sb("tf", [P, 2, NS])
        sidx = sb("sidx", [P, NS], I32)
        gidx = sb("gidx", [P, NS], I32)
        mp2 = sb("mp2", [P, 2, NS])
        area = sb("area", [P, QB * (NH + NG) * S // 2])

        def part(at, *shape):
            n = int(np.prod(shape))
            names = "abc"[:len(shape)]
            v = area[:, at:at + n]
            if len(shape) > 1:
                v = v.rearrange(f"p ({' '.join(names)}) -> p {' '.join(names)}",
                                **dict(zip(names, shape)))
            return v, at + n

        xg, used = part(0, XG, 2 * H)
        xT, used = part(used, 2, C, P)
        sil, used = part(used, 2, I)
        hh, used = part(used, 2, I)
        hT, used = part(used, 2, IC, P)
        ob, used = part(used, OB, H)
        q32 = sb("q32", [P, 2, S])
        qr = sb("qr", [P, 2, S])
        qp = sb("qp", [P, 3, 2, S], BF16)
        k32 = sb("k32", [NG * D, S])
        kr = sb("kr", [NG * D, S])
        kp = sb("kp", [NG * D, 3, S], BF16)
        half = QB * NH * S // 2
        Qs = area[:, 0:half].bitcast(BF16).rearrange("p (r h s) -> p r h s", r=QB, h=NH)
        Ks = area[:, half:].bitcast(BF16).rearrange("p (r h s) -> p r h s", r=QB, h=NG)
        V = sb("V", [P, QB, TB, NG, 2 * D])
        mxa = sb("mxa", [P, 2, TB, NH])
        nmx = sb("nmx", [P, TB, NH], BF16)
        mT = sb("mT", [NH, S], BF16)
        PT = sb("PT", [P, 2, 3 * 512])
        OT = sb("OT", [P, 2, S])
        rc = sb("rc", [P, TB, HG])
        at = sb("at", [P, TB, HG * D])

        bank = [ctx.enter_context(nc.psum_tensor(f"bank{i}", [P, 512], F32)) for i in range(8)]
        bankm = bank[7][:, 0:P].bitcast(BF16)

        def cst(name):
            return cf[:, CONST_AT[name]:CONST_AT[name] + CONST[name]]

        def cstb(name):
            return cb[:, CONSTB_AT[name]:CONSTB_AT[name] + CONSTB[name]]

        ident, identb = cst("ident"), cstb("identb")
        rsf = rs[:].bitcast(F32)

        s_x = [sem(f"s_x{b}") for b in range(B)]
        s_cst = sem("s_cst")
        s_w = sem("s_w")
        s_x2 = [sem(f"s_x2_{b}") for b in range(B)]
        s_const = sem("s_const")
        dve = sem("dve")
        pool = sem("pool")
        s_st = [sem(f"s_st{k}") for k in range(3)]
        s_rs = [sem(f"s_rs{k}") for k in range(3)]
        s_xn = [sem(f"s_xn{k}") for k in range(3)]
        s_xp = [sem(f"s_xp{k}") for k in range(3)]
        s_xs = [sem(f"s_xs{k}") for k in range(3)]
        s_row = [[sem(f"s_row{l}_{i}") for i in range(2)] for l in range(2)]
        s_lp = [sem(f"s_lp{l}") for l in range(2)]
        s_ls = [sem(f"s_ls{l}") for l in range(2)]
        s_ex = [sem(f"s_ex{l}") for l in range(2)]
        s_oh = [sem(f"s_oh{l}") for l in range(2)]
        s_rk = [sem(f"s_rk{l}") for l in range(2)]
        s_rj = [sem(f"s_rj{l}") for l in range(2)]
        s_sl = [sem(f"s_sl{l}") for l in range(2)]
        s_ix = [sem(f"s_ix{l}") for l in range(2)]
        f_g = [[sem(f"f_g{l}_{i}") for i in range(XG)] for l in range(2)]
        f_s = [[sem(f"f_s{l}_{i}") for i in range(OB)] for l in range(2)]
        f_xp = [sem(f"f_xp{l}") for l in range(2)]
        f_xs = [sem(f"f_xs{l}") for l in range(2)]
        f_gp = [sem(f"f_gp{l}") for l in range(2)]
        f_up = [sem(f"f_up{l}") for l in range(2)]
        f_si = [sem(f"f_si{l}") for l in range(2)]
        f_h = [sem(f"f_h{l}") for l in range(2)]
        f_hp = [sem(f"f_hp{l}") for l in range(2)]
        f_hs = [sem(f"f_hs{l}") for l in range(2)]
        f_y = [sem(f"f_y{l}") for l in range(2)]
        f_o = [sem(f"f_o{l}") for l in range(2)]
        a_q = sem("a_q")
        a_kv = sem("a_kv")
        a_q32 = sem("a_q32")
        a_k32 = sem("a_k32")
        a_v = sem("a_v")
        a_qh = sem("a_qh")
        a_qr = sem("a_qr")
        a_qm = sem("a_qm")
        a_ql = sem("a_ql")
        a_qd = sem("a_qd")
        a_qs = [sem(f"a_qs{i}") for i in range(QB)]
        a_a = sem("a_a")
        a_am = sem("a_am")
        a_nm = sem("a_nm")
        a_mp = sem("a_mp")
        a_ms = sem("a_ms")
        a_md = sem("a_md")
        a_mq = [sem(f"a_mq{i}") for i in range(QB)]
        a_st = sem("a_st")
        a_e = sem("a_e")
        a_pm = sem("a_pm")
        a_o = sem("a_o")
        a_os = sem("a_os")
        a_ot = sem("a_ot")
        a_x3 = sem("a_x3")
        s_out = sem("s_out")

        block = ctx.enter_context(nc.Block())

        def tiles(k, b):
            return (0, NT) if k == 0 else (TB * b, TB * b + TB)

        def ln_stats(k, b, seen):
            t0, t1 = tiles(k, b)
            for t in range(t0, t1):
                if k == 0 and t % TB == 0:
                    nc.vector.wait_ge(s_x[t // TB], 16)
                nc.vector.bn_stats(bn[:, t, :], xt[:, t, :]).then_inc(dve, 1)
            seen[0] += t1 - t0
            nc.vector.wait_ge(dve, seen[0])
            for t in range(t0, t1):
                nc.vector.bn_aggr(mv[:, t, :], bn[:, t, :]).then_inc(dve, 1)
            seen[0] += t1 - t0
            nc.vector.wait_ge(dve, seen[0])
            link(nc.vector.tensor_scalar(ve[:, t0:t1], mv[:, t0:t1, 1], EPS, None, ALU.add), seen)
            link(nc.vector.tensor_scalar(hv[:, t0:t1], ve[:, t0:t1].bitcast(I32), 1, None,
                                         ALU.arith_shift_right), seen)
            nc.vector.tensor_scalar(rs[:, t0:t1], hv[:, t0:t1], -1.0, RSQRT_MAGIC,
                                    ALU.mult, ALU.add).then_inc(s_st[k], 1)

        def link(ins, seen):
            seen[0] += 1
            ins.then_inc(dve, 1)
            nc.vector.wait_ge(dve, seen[0])

        def plink(ins, seen):
            seen[0] += 1
            ins.then_inc(pool, 1)
            nc.gpsimd.wait_ge(pool, seen[0])

        def ln_newton(k, b, seen):
            t0, t1 = tiles(k, b)
            v, r, n = ve[:, t0:t1], rsf[:, t0:t1], nw[:, t0:t1]
            nc.gpsimd.wait_ge(s_st[k], (b if k else 0) + 1)
            for step in range(3):
                plink(nc.gpsimd.tensor_tensor(n, r, r, ALU.mult), seen)
                plink(nc.gpsimd.tensor_tensor(n, n, v, ALU.mult), seen)
                plink(nc.gpsimd.tensor_scalar(n, n, -0.5, 1.5, ALU.mult, ALU.add), seen)
                last = nc.gpsimd.tensor_tensor(r, r, n, ALU.mult)
                if step < 2:
                    plink(last, seen)
            last.then_inc(s_rs[k], 1)

        def ln_apply(k, b):
            nc.vector.wait_ge(s_rs[k], (b if k else 0) + 1)
            dst = xn[:, b % 2] if k < 2 else xnr[:]
            if k == 0 and b >= 2:
                nc.vector.wait_ge(s_row[0][b % 2], 32 * (b // 2))
            if k == 2 and b >= 1:
                nc.vector.wait_ge(s_row[1][0], 32 * b)
            if k < 2 and b >= 2:
                nc.vector.wait_ge(s_xp[k], b - 1)
            if k == 2 and b >= 1:
                nc.vector.wait_ge(s_xp[k], b)
            for i in range(TB):
                t = TB * b + i
                nc.vector.tensor_scalar(dst[:, i, :], xt[:, t, :], mv[:, t, 0:1], rsf[:, t:t + 1],
                                        ALU.subtract, ALU.mult).then_inc(s_xn[k], 1)

        def ln_transpose(k, b, ps):
            src = xn[:, b % 2] if k < 2 else xnr[:]
            nc.tensor.wait_ge(s_xn[k], TB * (b + 1))
            o = ps[:].rearrange("p (c s) -> p c s", c=C)
            for i in range(TB):
                for c in range(C):
                    last = nc.tensor.transpose(o[:, c, i * P:(i + 1) * P],
                                               src[:, i, c * P:(c + 1) * P], ident)
            last.then_inc(s_xp[k], 1)

        def ln_evacuate(k, b, ps):
            nc.scalar.wait_ge(s_xp[k], b + 1)
            dst = xnT[:, b % 2] if k < 2 else xnrT[:]
            nc.scalar.copy(dst, ps[:].rearrange("p (c s) -> p c s", c=C)).then_inc(s_xs[k], 1)

        def logits(l, b, ps):
            k = 2 * l
            src = xnT[:, b % 2] if k < 2 else xnrT[:]
            nc.tensor.wait_ge(s_xs[k], b + 1)
            for i in range(TB):
                for c in range(C):
                    last = nc.tensor.matmul(ps[:, i * NE:(i + 1) * NE], src[:, c, i * P:(i + 1) * P],
                                            wr[:, c, :], start=(c == 0), stop=(c == C - 1))
            last.then_inc(s_lp[l], 1)

        def logits_copy(l, b, ps):
            nc.vector.wait_ge(s_lp[l], b + 1)
            nc.vector.tensor_copy(lg[:, TB * b:TB * b + TB, :],
                                  ps[:, 0:TB * NE].rearrange("p (t e) -> p t e", e=NE)).then_inc(s_ls[l], 1)

        def rows_written(eng, l):
            if l == 0:
                eng.wait_ge(s_row[0][0], 32 * (B // 2))
                eng.wait_ge(s_row[0][1], 32 * (B // 2))
            else:
                eng.wait_ge(s_row[1][0], 32 * B)

        def write_rows(eng, l, b):
            k = 2 * l
            src = xn[:, b % 2] if k < 2 else xnr[:]
            dst = rows[l][S * b:S * b + S, :].rearrange("(t p) f -> p t f", p=P)
            eng.wait_ge(s_xn[k], TB * (b + 1))
            done = s_row[0][b % 2] if l == 0 else s_row[1][0]
            eng.dma_start(dst[:, :, 0:H], xt[:, TB * b:TB * b + TB, :]).then_inc(done, 16)
            eng.dma_start(dst[:, :, H:2 * H], src).then_inc(done, 16)

        def route_dve(l, seen):
            v = nc.vector
            v.wait_ge(s_ex[l], 1)
            link(v.tensor_scalar(sg[:], sg[:], 1.0, None, ALU.add), seen)
            link(v.reciprocal(sg[:], sg[:]), seen)
            link(v.tensor_reduce(mx[:], sg[:], AX.X, ALU.max), seen)
            link(v.tensor_tensor(eq[:], sg[:], mx[:].unsqueeze(2).to_broadcast([P, NT, NE]), ALU.is_equal), seen)
            desc = cst("desc").unsqueeze(1).to_broadcast([P, NT, NE])
            link(v.tensor_tensor(eq[:], eq[:], desc, ALU.mult), seen)
            link(v.tensor_reduce(pm[:], eq[:], AX.X, ALU.max), seen)
            v.tensor_tensor(oh[:], desc, pm[:].unsqueeze(2).to_broadcast([P, NT, NE]),
                            ALU.is_equal).then_inc(s_oh[l], 1)
            link(v.tensor_copy(mh[:, :, 0], mx[:]), seen)
            link(v.tensor_tensor(mr[:], mx[:], mh[:, :, 0], ALU.subtract), seen)
            link(v.tensor_copy(mh[:, :, 1], mr[:]), seen)
            v.tensor_copy(vals[:, :, 0:2], cst("toks").rearrange("p (t k) -> p t k", k=2)).then_inc(dve, 1)
            v.tensor_copy(vals[:, :, 2:4], mh[:]).then_inc(dve, 1)
            v.tensor_tensor(vals[:, :, 4], mr[:], mh[:, :, 1], ALU.subtract).then_inc(dve, 1)
            seen[0] += 3
            v.wait_ge(s_rk[l], 1)
            link(v.tensor_copy(tot[:], bank[4][:, P:P + NE]), seen)
            link(v.tensor_tensor(tgt[:], tot[:].unsqueeze(2).to_broadcast([P, NE, NT]),
                                 cst("c128")[:, 0:NT].unsqueeze(1).to_broadcast([P, NE, NT]), ALU.is_gt), seen)
            link(v.tensor_reduce(ntl[:], tgt[:], AX.X, ALU.add), seen)
            link(v.tensor_tensor(lw[:], ntl[:].unsqueeze(1).to_broadcast([P, NE, NE]),
                                 cst("lower").rearrange("p (e f) -> p e f", e=NE), ALU.mult), seen)
            link(v.tensor_reduce(bt[:, 0, :], lw[:], AX.X, ALU.add), seen)
            v.tensor_tensor(bt[:, 1, :], bt[:, 0, :], ntl[:], ALU.add).then_inc(dve, 1)
            seen[0] += 1
            link(v.tensor_scalar(bt[:, 2, :], bt[:, 0, :], float(P), None, ALU.mult), seen)
            link(v.tensor_tensor(rk[:], bank[4][:, 0:P].rearrange("p (t e) -> p t e", e=NE),
                                 bt[:, 2, :].unsqueeze(1).to_broadcast([P, NT, NE]), ALU.add), seen)
            link(v.tensor_tensor(rk[:], rk[:], oh[:], ALU.mult), seen)
            link(v.tensor_reduce(pos[:], rk[:], AX.X, ALU.add), seen)
            link(v.tensor_tensor(gj[:], pos[:].unsqueeze(2).to_broadcast([P, NT, NS + 1]),
                                 cst("c128").unsqueeze(1).to_broadcast([P, NT, NS + 1]), ALU.is_ge), seen)
            v.tensor_tensor(J[:], gj[:, :, 0:NS], gj[:, :, 1:NS + 1], ALU.subtract).then_inc(dve, 1)
            seen[0] += 1
            link(v.tensor_reduce(jt[:, 0, :], gj[:], AX.X, ALU.add), seen)
            link(v.tensor_scalar(jt[:, 1, :], jt[:, 0, :], -float(P), float(P), ALU.mult, ALU.add), seen)
            link(v.tensor_tensor(rb[:], pos[:], jt[:, 1, :], ALU.add), seen)
            h = NT // 2
            for t in (0, h):
                v.tensor_tensor(R1[:, t:t + h, :], cstb("iota").unsqueeze(1).to_broadcast([P, h, P]),
                                rb[:, t:t + h].unsqueeze(2).to_broadcast([P, h, P]),
                                ALU.is_equal).then_inc(s_rj[l], 1)
                v.tensor_tensor(J5[:, t:t + h], J[:, t:t + h, :].unsqueeze(2).to_broadcast([P, h, 5, NS]),
                                vals[:, t:t + h, :].unsqueeze(3).to_broadcast([P, h, 5, NS]),
                                ALU.mult).then_inc(s_rj[l], 1)
            link(v.tensor_tensor(eg[:], bt[0:1, 1, :].unsqueeze(1).to_broadcast([1, NS, NE]),
                                 cst("jrow")[0:1, :].unsqueeze(2).to_broadcast([1, NS, NE]), ALU.is_le), seen)
            link(v.tensor_reduce(ef[:, 0, :], eg[:], AX.X, ALU.add), seen)
            v.tensor_scalar(ef[:, 1, :], ef[:, 0, :], float(NE - 1), float(WE), ALU.min, ALU.mult).then_inc(dve, 1)
            seen[0] += 1
            v.wait_ge(dve, seen[0])
            v.tensor_copy(eoff[:], ef[:, 1, :]).then_inc(s_ix[l], 1)
            v.wait_ge(s_sl[l], 1)
            link(v.tensor_copy(sl[:], bank[5][:, 0:5 * NS].rearrange("p (k j) -> p k j", k=5)), seen)
            link(v.scalar_tensor_tensor(out=tf[:, 0, :], in0=sl[:, 0, :], scalar=float(PAD), in1=sl[:, 1, :],
                                        op0=ALU.add, op1=ALU.add), seen)
            v.tensor_copy(sidx[:], tf[:, 0, :]).then_inc(s_ix[l], 1)
            v.tensor_scalar(gidx[:], tf[:, 0, :], float(T - 1), None, ALU.min).then_inc(s_ix[l], 1)
            link(v.tensor_tensor(mp2[:, 0, :], sl[:, 2, :], sl[:, 3, :], ALU.add), seen)
            link(v.tensor_tensor(mp2[:, 0, :], mp2[:, 0, :], sl[:, 4, :], ALU.add), seen)
            link(v.tensor_scalar(mp2[:, 1, :], mp2[:, 0, :], 0.5, None, ALU.mult), seen)

        def route_act(l):
            nc.scalar.wait_ge(s_ls[l], B)
            nc.scalar.activation(sg[:], lg[:], ACT.Exp, scale=-1.0).then_inc(s_ex[l], 1)

        def route_pe(l):
            pe = nc.tensor
            pe.wait_ge(s_oh[l], 1)
            o2 = oh[:].rearrange("p t e -> p (t e)")
            pe.matmul(bank[4][:, 0:P], cstb("before"), o2, start=True, stop=False)
            for s in range(1, NT):
                pe.matmul(bank[4][:, s * NE:P], cstb("ones"), o2[:, 0:P - s * NE],
                          start=False, stop=(s == NT - 1))
            for t in range(NT):
                last = pe.matmul(bank[4][:, P:P + NE], cstb("ones"), oh[:, t, :],
                                 start=(t == 0), stop=(t == NT - 1))
            last.then_inc(s_rk[l], 1)
            for t in range(NT):
                if t % (NT // 2) == 0:
                    pe.wait_ge(s_rj[l], 2 if t == 0 else 4)
                last = pe.matmul(bank[5][:, 0:5 * NS], R1[:, t, :],
                                 J5[:, t].rearrange("p k j -> p (k j)"), start=(t == 0), stop=(t == NT - 1))
            last.then_inc(s_sl[l], 1)

        def gather(l, j, k):
            nc.gpsimd.indirect_dma_start(
                xg[:, k % XG, :], None, rows[l],
                bass.IndirectOffsetOnAxis(ap=gidx[:, bass.ds(j, 1)], axis=0)).then_inc(f_g[l][k % XG], 16)

        def scatter(l, j, k):
            nc.gpsimd.indirect_dma_start(
                ffn_out[l], bass.IndirectOffsetOnAxis(ap=sidx[:, bass.ds(j, 1)], axis=0),
                ob[:, k % OB, :], None, bounds_check=T - 1, oob_is_err=False).then_inc(f_s[l][k % OB], 16)

        def scattered(eng, l):
            for i in range(OB):
                eng.wait_ge(f_s[l][i], 16 * ((NS - 1 - i) // OB + 1))

        def ffn_pool(l):
            p = nc.gpsimd
            p.wait_ge(s_ix[l], 3)
            rows_written(p, l)
            for j in range(min(XG, NS)):
                gather(l, j, j)
            for j in range(1, NS + 1):
                p.wait_ge(f_o[l], j)
                scatter(l, j - 1, j - 1)
                if j + XG - 1 < NS:
                    gather(l, j + XG - 1, j + XG - 1)

        def ffn_pe_step(l, j, k):
            pe = nc.tensor
            if 1 <= j:
                pe.wait_ge(f_h[l], j)
                if j >= 2:
                    pe.wait_ge(f_hs[l], j - 1)
                for i in range(IC):
                    last = pe.transpose(bank[4][:, i * P:(i + 1) * P],
                                        hh[:, (k - 1) % 2, i * P:(i + 1) * P], ident)
                last.then_inc(f_hp[l], 1)
            for n in ([0, 1] if j == 0 else [j + 1]):
                if n < NS:
                    pe.wait_ge(f_g[l][n % XG], 16 * (n // XG + 1))
                    if n >= 1:
                        pe.wait_ge(f_xs[l], n)
                    for c in range(C):
                        last = pe.transpose(bank[5][:, c * P:(c + 1) * P],
                                            xg[:, n % XG, H + c * P:H + (c + 1) * P], ident)
                    last.then_inc(f_xp[l], 1)
            if j < NS:
                pe.wait_ge(f_xs[l], j + 1)
                if j >= 2:
                    pe.wait_ge(f_si[l], j - 1)
                    pe.wait_ge(f_h[l], j - 1)
                off = pe.value_load(eoff[0:1, bass.ds(j, 1)], min_val=0, max_val=(NE - 1) * WE)
                for m, done in ((0, f_gp), (1, f_up)):
                    for c in range(C):
                        last = pe.matmul(bank[2 * m + k % 2][:], xT[:, k % 2, c, :],
                                         W[:, bass.ds(off + (m * C + c) * I, I)],
                                         start=(c == 0), stop=(c == C - 1))
                    last.then_inc(done[l], 1)
            if j >= 1:
                pe.wait_ge(f_hs[l], j)
                if j >= 3:
                    pe.wait_ge(f_o[l], j - 2)
                off = pe.value_load(eoff[0:1, bass.ds(j - 1, 1)], min_val=0, max_val=(NE - 1) * WE)
                for i in range(IC):
                    last = pe.matmul(bank[6 + (k - 1) % 2][:, 0:H], hT[:, (k - 1) % 2, i, :],
                                     W[:, bass.ds(off + 2 * C * I + i * H, H)],
                                     start=(i == 0), stop=(i == IC - 1))
                last.then_inc(f_y[l], 1)

        def ffn_act_step(l, j, k):
            a = nc.scalar
            if j >= 1:
                a.wait_ge(f_hp[l], j)
                if j >= 3:
                    a.wait_ge(f_y[l], j - 2)
                a.copy(hT[:, (k - 1) % 2], bank[4][:].rearrange("p (i s) -> p i s", i=IC)).then_inc(f_hs[l], 1)
            if j < NS:
                a.wait_ge(f_gp[l], j + 1)
                if j >= 2:
                    a.wait_ge(f_h[l], j - 1)
                a.activation(sil[:, k % 2, :], bank[k % 2][:], ACT.Silu).then_inc(f_si[l], 1)

        def ffn_dve_step(l, j, k):
            v = nc.vector
            for n in ([0, 1] if j == 0 else [j + 1]):
                if n < NS:
                    v.wait_ge(f_xp[l], n + 1)
                    if n >= 2:
                        v.wait_ge(f_up[l], n - 1)
                    v.tensor_copy(xT[:, n % 2], bank[5][:, 0:H].rearrange("p (c s) -> p c s", c=C)).then_inc(f_xs[l], 1)
            if j < NS:
                v.wait_ge(f_si[l], j + 1)
                v.wait_ge(f_up[l], j + 1)
                if j >= 2:
                    v.wait_ge(f_hp[l], j - 1)
                v.tensor_tensor(hh[:, k % 2, :], sil[:, k % 2, :], bank[2 + k % 2][:], ALU.mult).then_inc(f_h[l], 1)
            if j >= 1:
                v.wait_ge(f_y[l], j)
                if j > OB:
                    v.wait_ge(f_s[l][(j - 1) % OB], 16 * ((j - 1) // OB))
                v.scalar_tensor_tensor(out=ob[:, (k - 1) % OB, :], in0=bank[6 + (k - 1) % 2][:, 0:H],
                                       scalar=mp2[:, 1, bass.ds(j - 1, 1)], in1=xg[:, (k - 1) % XG, 0:H],
                                       op0=ALU.mult, op1=ALU.add).then_inc(f_o[l], 1)

        def a_proj_q(b):
            pe = nc.tensor
            pe.wait_ge(s_xs[1], b + 1)
            for m in range(2):
                for c in range(C):
                    last = pe.matmul(bank[7][:, m * S:(m + 1) * S], wq_s[:, c, m * P:(m + 1) * P],
                                     xnT[:, b % 2, c, :], start=(c == 0), stop=(c == C - 1))
            last.then_inc(a_q, 1)

        def a_proj_kv(b):
            pe = nc.tensor
            for c in range(C):
                pe.matmul(bank[6][0:NG * D, 0:S], wk_s[:, c, :], xnT[:, b % 2, c, :],
                          start=(c == 0), stop=(c == C - 1))
            for i in range(TB):
                for c in range(C):
                    last = pe.matmul(bank[6][:, S + i * NG * D:S + (i + 1) * NG * D],
                                     xnT[:, b % 2, c, i * P:(i + 1) * P], wv_s[:, c, :],
                                     start=(c == 0), stop=(c == C - 1))
            last.then_inc(a_kv, 1)

        def a_split_act(b):
            a = nc.scalar
            a.wait_ge(a_q, b + 1)
            if b >= 1:
                a.wait_ge(a_qr, 2 * b)
            for m in range(2):
                last = a.activation(q32[:, m, :], bank[7][:, m * S:(m + 1) * S], ACT.Identity,
                                    bias=bq_s[:, m:m + 1])
            last.then_inc(a_q32, 1)

        def a_split_act2(b):
            a = nc.scalar
            a.wait_ge(a_q32, b + 1)
            a.wait_ge(a_k32, b + 1)
            if b >= 1:
                a.wait_ge(a_qd, 32 * b)
            a.copy(qp[:, 0], q32[:])
            a.copy(kp[:, 0], k32[:]).then_inc(a_qh, 1)

        def a_split_act3(b):
            a = nc.scalar
            a.wait_ge(a_qr, 2 * b + 2)
            a.copy(qp[:, 1], qr[:])
            a.copy(kp[:, 1], kr[:]).then_inc(a_qm, 1)

        def a_split_dve(b):
            v = nc.vector
            v.wait_ge(a_kv, b + 1)
            v.tensor_scalar(k32[:], bank[6][0:NG * D, 0:S], bk_s[:], None, ALU.add).then_inc(a_k32, 1)
            v.tensor_tensor(V[:, b % QB, :, :, 0:D],
                            bank[6][:, S:S + TB * NG * D].rearrange("p (t g d) -> p t g d", t=TB, g=NG),
                            bv_s[:].rearrange("p (g d) -> p g d", g=NG).unsqueeze(1).to_broadcast([P, TB, NG, D]),
                            ALU.add).then_inc(a_v, 1)

        def a_split_dve2(b):
            v = nc.vector
            v.wait_ge(a_qh, b + 1)
            v.tensor_tensor(qr[:], q32[:], qp[:, 0], ALU.subtract).then_inc(a_qr, 1)
            v.tensor_tensor(kr[:], k32[:], kp[:, 0], ALU.subtract).then_inc(a_qr, 1)

        def a_split_dve3(b):
            v = nc.vector
            v.wait_ge(a_qm, b + 1)
            v.tensor_tensor(qp[:, 2], qr[:], qp[:, 1], ALU.subtract).then_inc(a_ql, 1)
            v.tensor_tensor(kp[:, 2], kr[:], kp[:, 1], ALU.subtract).then_inc(a_ql, 1)

        def a_stack(sp, b):
            r = b % QB
            sp.wait_ge(a_ql, 2 * b + 2)
            sp.dma_start(qd[r].rearrange("k (m p) s -> p k m s", p=P), qp[:]).then_inc(a_qd, 16)
            sp.dma_start(kd[r].rearrange("k p s -> p k s"), kp[:]).then_inc(a_qd, 16)
            sp.wait_ge(a_qd, 32 * (b + 1))
            if b >= QB:
                sp.wait_ge(a_st, 3 * NG * (b - QB + 1))
            for i, (pq, pk) in enumerate(zip(Q_PART, K_PART)):
                sp.dma_start(Qs[D * i:D * i + D, r], qd[r, pq].rearrange("(h d) s -> d h s", d=D)).then_inc(a_qs[r], 16)
                sp.dma_start(Ks[D * i:D * i + D, r], kd[r, pk].rearrange("(h d) s -> d h s", d=D)).then_inc(a_qs[r], 16)

        def a_max_row(sp, b):
            r = b % QB
            sp.wait_ge(a_ms, b + 1)
            sp.dma_start(md[r], mT[:]).then_inc(a_md, 16)
            sp.wait_ge(a_md, 16 * (b + 1))
            sp.dma_start(Qs[KROWS:KROWS + 1, r], md[r:r + 1]).then_inc(a_mq[r], 16)

        def a_max_pe(b, g):
            pe = nc.tensor
            r = b % QB
            if g == 0:
                pe.wait_ge(a_qs[r], 32 * len(Q_PART) * (b // QB + 1))
            for u in range(3):
                n = 3 * (NG * b + g) + u
                if n >= 2:
                    pe.wait_ge(a_am, n - 1)
                o = bank[3 + n % 2]
                if u == 0:
                    for h in range(HG):
                        pe.matmul(o[:, h * P:(h + 1) * P], Qs[0:KROWS, r, HG * g + h, 0:P],
                                  Ks[0:KROWS, r, g, 0:P], start=(h == 0), stop=False)
                    last = pe.matmul(o[:], identb, cstb("mask"), start=False, stop=True)
                else:
                    for h in range(2):
                        pe.matmul(o[:, h * S:(h + 1) * S], Qs[0:KROWS, r, HG * g + 2 * (u - 1) + h, P:S],
                                  Ks[0:KROWS, r, g, :], start=(h == 0), stop=False)
                    last = pe.matmul(o[:].rearrange("p (h k) -> p h k", h=2)[:, :, P:S], identb,
                                     cstb("mask")[:, 0:2 * P].rearrange("p (h k) -> p h k", h=2),
                                     start=False, stop=True)
                last.then_inc(a_a, 1)

        def a_max_dve(b, g):
            v = nc.vector
            for u in range(3):
                n = 3 * (NG * b + g) + u
                v.wait_ge(a_a, n + 1)
                o = bank[3 + n % 2]
                if u == 0:
                    v.tensor_reduce(mxa[:, b % 2, 0, HG * g:HG * g + HG],
                                    o[:].rearrange("p (h k) -> p h k", h=HG), AX.X, ALU.max).then_inc(a_am, 1)
                else:
                    h0 = HG * g + 2 * (u - 1)
                    v.tensor_reduce(mxa[:, b % 2, 1, h0:h0 + 2],
                                    o[:].rearrange("p (h k) -> p h k", h=2), AX.X, ALU.max).then_inc(a_am, 1)

        def a_neg_dve(b):
            v = nc.vector
            v.wait_ge(a_am, 3 * NG * (b + 1))
            if b >= 1:
                v.wait_ge(a_mp, b)
            v.tensor_scalar(nmx[:], mxa[:, b % 2], -1.0, None, ALU.mult).then_inc(a_nm, 1)

        def a_neg_pe(b):
            pe = nc.tensor
            pe.wait_ge(a_nm, b + 1)
            if b >= 1:
                pe.wait_ge(a_x3, NG * (b - 1) + 1)
            for i in range(TB):
                last = pe.transpose(bankm[0:NH, i * P:(i + 1) * P], nmx[:, i, :], identb)
            last.then_inc(a_mp, 1)

        def a_neg_copy(b):
            v = nc.vector
            v.wait_ge(a_mp, b + 1)
            if b >= 1:
                v.wait_ge(a_md, 16 * b)
            v.tensor_copy(mT[:], bankm[0:NH, 0:S]).then_inc(a_ms, 1)

        def a_scores(b, g):
            pe = nc.tensor
            r = b % QB
            n = NG * b + g
            if g == 0:
                pe.wait_ge(a_mq[r], 16 * (b // QB + 1))
            for u in range(3):
                if n >= 1:
                    pe.wait_ge(a_e, 3 * (n - 1) + u + 1)
                if u < 2:
                    rhs = Qs[0:KROWS + 1, r, HG * g + 2 * u:HG * g + 2 * u + 2, :]
                    o = bank[u][:].rearrange("p (h q) -> p h q", h=2)
                    k0 = 0
                else:
                    rhs = Qs[0:KROWS + 1, r, HG * g:HG * g + HG, P:S]
                    o = bank[u][:].rearrange("p (h q) -> p h q", h=HG)
                    k0 = P
                pe.matmul(o, Ks[0:KROWS + 1, r, g, k0:k0 + P], rhs, start=True, stop=True).then_inc(a_st, 1)

        def a_exp(b, g):
            a = nc.scalar
            n = NG * b + g
            for u in range(3):
                a.wait_ge(a_st, 3 * n + u + 1)
                if u == 0 and n >= 2:
                    a.wait_ge(a_o, n - 1)
                a.activation(PT[:, n % 2, u * 512:(u + 1) * 512], bank[u][:], ACT.Exp,
                             scale=D ** -0.5).then_inc(a_e, 1)

        def a_mask(b, g):
            p = nc.gpsimd
            n = NG * b + g
            for u, src in ((2, PT[:, n % 2, 0:1024].rearrange("p (h q) -> p h q", h=HG)[:, :, 0:P]),
                           (3, PT[:, n % 2, 1024:1536].rearrange("p (h q) -> p h q", h=HG))):
                p.wait_ge(a_e, 3 * n + u)
                p.affine_select(out=src, in_=src, compare_op=ALU.is_ge, fill=0.0, base=0,
                                pattern=[[0, HG], [1, P]], channel_multiplier=-1).then_inc(a_pm, 1)

        def a_values(b, g):
            pe = nc.tensor
            n = NG * b + g
            pe.wait_ge(a_pm, 2 * n + 2)
            pe.wait_ge(a_v, b + 1)
            if n >= 2:
                pe.wait_ge(a_os, n - 1)
            c0 = (n % 2) * S
            for h in range(HG):
                pe.matmul(bank[5][32 * h:32 * h + 32, c0:c0 + S], V[:, b % QB, 0, g, :],
                          PT[:, n % 2, h * S:(h + 1) * S], start=True, stop=False, tile_position=(0, 32 * h))
            for h in range(HG):
                last = pe.matmul(bank[5][32 * h:32 * h + 32, c0 + P:c0 + S], V[:, b % QB, 1, g, :],
                                 PT[:, n % 2, 1024 + h * P:1024 + (h + 1) * P], start=False, stop=True,
                                 tile_position=(0, 32 * h))
            last.then_inc(a_o, 1)

        def a_values_copy(b, g):
            a = nc.scalar
            n = NG * b + g
            a.wait_ge(a_o, n + 1)
            if n >= 2:
                a.wait_ge(a_ot, n - 1)
            a.copy(OT[:, n % 2, :], bank[5][:, (n % 2) * S:(n % 2) * S + S]).then_inc(a_os, 1)

        def a_heads_pe(b, g):
            pe = nc.tensor
            n = NG * b + g
            pe.wait_ge(a_os, n + 1)
            if n >= 1:
                pe.wait_ge(a_x3, n)
            if g == 0 and b + 1 < B:
                pe.wait_ge(a_q32, min(b + 2, B))
            for i in range(TB):
                last = pe.transpose(bank[7][:, i * P:(i + 1) * P], OT[:, n % 2, i * P:(i + 1) * P], ident)
            last.then_inc(a_ot, 1)

        def a_heads_dve(b, g, seen):
            v = nc.vector
            n = NG * b + g
            v.wait_ge(a_ot, n + 1)
            o = bank[7][:, 0:S].rearrange("p (t h d) -> p t h d", t=TB, h=HG)
            link(v.reciprocal(rc[:], o[:, :, :, D]), seen)
            link(v.tensor_tensor(at[:].rearrange("p t (h d) -> p t h d", h=HG), o[:, :, :, 0:D],
                                 rc[:].unsqueeze(3).to_broadcast([P, TB, HG, D]), ALU.mult), seen)
            xs = xt[:, TB * b:TB * b + TB, HG * D * g:HG * D * (g + 1)]
            v.tensor_tensor(xs, xs, at[:], ALU.add).then_inc(a_x3, 1)

        @block.sync
        def _(sp):
            for b in range(B):
                sp.dma_start(xt[:, TB * b:TB * b + TB, :],
                             x[S * b:S * b + S, :].rearrange("(t p) f -> p t f", p=P)).then_inc(s_x[b], 16)
            for e in range(NE):
                w = W[:, e * WE:(e + 1) * WE]
                for m, src in enumerate((gate[e], up[e])):
                    sp.dma_start(w[:, m * C * I:(m + 1) * C * I].rearrange("p (c n) -> p c n", c=C),
                                 src.rearrange("(c p) n -> p c n", p=P)).then_inc(s_w, 16)
                sp.dma_start(w[:, 2 * C * I:].rearrange("p (i n) -> p i n", i=IC),
                             down[e].rearrange("(i p) n -> p i n", p=P)).then_inc(s_w, 16)
            scattered(sp, 0)
            rows_written(sp, 0)
            for b in range(B):
                sp.dma_start(xt[:, TB * b:TB * b + TB, :],
                             x2d[S * b:S * b + S, :].rearrange("(t p) f -> p t f", p=P)).then_inc(s_x2[b], 16)
            a_stack(sp, 0)
            a_stack(sp, 1)
            a_max_row(sp, 0)
            for b in range(B):
                if b + 1 < B:
                    a_max_row(sp, b + 1)
                if b + 2 < B:
                    a_stack(sp, b + 2)

        @block.gpsimd
        def _(p):
            seen = [0]
            nc.gpsimd.memset(V[:], 0.0).then_inc(s_const, 1)
            p.wait_ge(s_const, 1)
            nc.gpsimd.memset(V[:, :, :, :, D:D + 1], 1.0).then_inc(s_const, 1)
            ln_newton(0, 0, seen)
            ffn_pool(0)
            scattered(p, 0)
            nc.gpsimd.memset(Ks[KROWS:KROWS + 1], 1.0).then_inc(s_const, 1)
            p.wait_ge(s_const, 3)
            ln_newton(1, 0, seen)
            ln_newton(1, 1, seen)
            for b in range(B):
                for g in range(NG):
                    a_mask(b, g)
                    if g == 0 and b + 2 < B:
                        ln_newton(1, b + 2, seen)
                    if g == 1 and b >= 1:
                        ln_newton(2, b - 1, seen)
            ln_newton(2, B - 1, seen)
            ffn_pool(1)
            scattered(p, 1)

        @block.scalar
        def _(a):
            for dst, src in ((cf[:], constf), (cb[:], constb),
                             (wr[:], router.rearrange("(c p) e -> p c e", p=P)),
                             (wq_s[:], wq.rearrange("(c p) e -> p c e", p=P)),
                             (wk_s[:], wk.rearrange("(c p) e -> p c e", p=P)),
                             (wv_s[:], wv.rearrange("(c p) e -> p c e", p=P)),
                             (bq_s[:], bq), (bk_s[:], bk), (bv_s[:], bv)):
                a.dma_start(dst, src).then_inc(s_cst, 16)
            for b in range(B):
                if b >= 2:
                    a.wait_ge(s_lp[0], b - 1)
                ln_evacuate(0, b, bank[6 + b % 2])
                write_rows(a, 0, b)
            route_act(0)
            for j in range(NS + 1):
                ffn_act_step(0, j, j)
            for b in range(2):
                ln_evacuate(1, b, bank[6])
                a_split_act(b)
                a_split_act2(b)
                a_split_act3(b)
            for b in range(B):
                for g in range(NG):
                    a_exp(b, g)
                    if g >= 1:
                        a_values_copy(b, g - 1)
                    if g == 1 and b + 2 < B:
                        ln_evacuate(1, b + 2, bank[6])
                    if g == 2 and b >= 1:
                        ln_evacuate(2, b - 1, bank[6])
                        write_rows(a, 1, b - 1)
                    if g == 2 and b + 2 < B:
                        a_split_act(b + 2)
                    if g == 3 and b + 2 < B:
                        a_split_act2(b + 2)
                a_values_copy(b, NG - 1)
                if b + 2 < B:
                    a_split_act3(b + 2)
            ln_evacuate(2, B - 1, bank[6])
            write_rows(a, 1, B - 1)
            route_act(1)
            for j in range(NS + 1):
                ffn_act_step(1, j, j)

        @block.vector
        def _(v):
            seen = [0]
            ln_stats(0, 0, seen)
            for b in range(B):
                ln_apply(0, b)
                if b >= 1:
                    logits_copy(0, b - 1, bank[4 + (b - 1) % 2])
            logits_copy(0, B - 1, bank[4 + (B - 1) % 2])
            v.wait_ge(s_cst, 16 * 9)
            route_dve(0, seen)
            for j in range(NS + 1):
                ffn_dve_step(0, j, j)
            for b in range(2):
                v.wait_ge(s_x2[b], 16)
                ln_stats(1, b, seen)
                ln_apply(1, b)
                if b == 0:
                    v.wait_ge(s_const, 3)
                a_split_dve(b)
                a_split_dve2(b)
                a_split_dve3(b)
            for g in range(NG):
                a_max_dve(0, g)
            a_neg_dve(0)
            a_neg_copy(0)
            for b in range(B):
                if b + 2 < B:
                    v.wait_ge(s_x2[b + 2], 16)
                    ln_stats(1, b + 2, seen)
                if b + 1 < B:
                    a_max_dve(b + 1, 0)
                    a_max_dve(b + 1, 1)
                if b + 2 < B:
                    ln_apply(1, b + 2)
                if b >= 1:
                    ln_apply(2, b - 1)
                if b + 1 < B:
                    a_max_dve(b + 1, 2)
                    a_max_dve(b + 1, 3)
                    a_neg_dve(b + 1)
                a_heads_dve(b, 0, seen)
                if b + 1 < B:
                    a_neg_copy(b + 1)
                a_heads_dve(b, 1, seen)
                if b >= 1:
                    logits_copy(1, b - 1, bank[6])
                if b + 2 < B:
                    a_split_dve(b + 2)
                    a_split_dve2(b + 2)
                a_heads_dve(b, 2, seen)
                if b + 2 < B:
                    a_split_dve3(b + 2)
                a_heads_dve(b, 3, seen)
                v.wait_ge(a_x3, NG * (b + 1))
                ln_stats(2, b, seen)
            ln_apply(2, B - 1)
            logits_copy(1, B - 1, bank[6])
            route_dve(1, seen)
            for j in range(NS + 1):
                ffn_dve_step(1, j, j)

        @block.tensor
        def _(pe):
            pe.wait_ge(s_cst, 16 * 9)
            for b in range(B):
                if b >= 2:
                    pe.wait_ge(s_xs[0], b - 1)
                ln_transpose(0, b, bank[6 + b % 2])
                if b >= 1:
                    if b >= 3:
                        pe.wait_ge(s_ls[0], b - 2)
                    logits(0, b - 1, bank[4 + (b - 1) % 2])
            pe.wait_ge(s_ls[0], B - 2)
            logits(0, B - 1, bank[4 + (B - 1) % 2])
            pe.wait_ge(s_ls[0], B)
            route_pe(0)
            pe.wait_ge(s_w, 48 * NE)
            pe.wait_ge(s_ix[0], 3)
            for j in range(NS + 1):
                ffn_pe_step(0, j, j)
            pe.wait_ge(s_const, 3)
            pe.wait_ge(f_o[0], NS)
            for b in range(2):
                if b:
                    pe.wait_ge(a_k32, b)
                    pe.wait_ge(a_v, b)
                    pe.wait_ge(a_q32, b)
                ln_transpose(1, b, bank[6])
                a_proj_q(b)
                a_proj_kv(b)
            for g in range(NG):
                a_max_pe(0, g)
            pe.wait_ge(a_q32, 2)
            a_neg_pe(0)
            for b in range(B):
                pe.wait_ge(a_ms, b + 1)
                a_scores(b, 0)
                if b + 1 < B:
                    a_max_pe(b + 1, 0)
                    a_max_pe(b + 1, 1)
                if b + 2 < B:
                    if b >= 2:
                        pe.wait_ge(s_ls[1], b - 1)
                    pe.wait_ge(a_v, b + 2)
                    ln_transpose(1, b + 2, bank[6])
                a_scores(b, 1)
                a_values(b, 0)
                if b + 1 < B:
                    a_max_pe(b + 1, 2)
                    a_max_pe(b + 1, 3)
                a_heads_pe(b, 0)
                a_scores(b, 2)
                a_values(b, 1)
                if b + 1 < B:
                    pe.wait_ge(a_x3, NG * b + 1)
                    a_neg_pe(b + 1)
                if b >= 1:
                    if b + 2 < B:
                        pe.wait_ge(s_xs[1], b + 3)
                    else:
                        pe.wait_ge(a_v, B)
                        pe.wait_ge(a_k32, B)
                    if b >= 2:
                        pe.wait_ge(s_ls[1], b - 1)
                    ln_transpose(2, b - 1, bank[6])
                if b + 1 < B:
                    pe.wait_ge(a_ms, b + 2)
                a_heads_pe(b, 1)
                a_scores(b, 3)
                a_values(b, 2)
                if b + 2 < B:
                    pe.wait_ge(a_x3, NG * b + 2)
                    a_proj_q(b + 2)
                if b >= 1:
                    logits(1, b - 1, bank[6])
                if b + 2 < B:
                    if b >= 1:
                        pe.wait_ge(s_ls[1], b)
                    a_proj_kv(b + 2)
                    pe.wait_ge(a_q32, b + 3)
                a_heads_pe(b, 2)
                a_values(b, 3)
                a_heads_pe(b, 3)
            ln_transpose(2, B - 1, bank[6])
            logits(1, B - 1, bank[6])
            pe.wait_ge(s_ls[1], B)
            route_pe(1)
            pe.wait_ge(s_ix[1], 3)
            for j in range(NS + 1):
                ffn_pe_step(1, j, j)


def kernel(**inputs):
    import concourse.bacc as bacc
    from concourse.bass_utils import run_bass_kernel_spmd

    a = {k: np.asarray(v) for k, v in inputs.items()}
    cf, cbf = constants()
    import ml_dtypes
    by_head = lambda w: np.ascontiguousarray(w.transpose(1, 0, 2).reshape(H, -1))
    arrays = {
        "x": a["L0_attn_x"].reshape(T, H),
        "wq": by_head(a["L0_attn_Wq"]),
        "bq": np.ascontiguousarray(a["L0_attn_bq"].reshape(2, P).T),
        "wk": by_head(a["L0_attn_Wk"]),
        "bk": a["L0_attn_bk"].reshape(NG * D, 1),
        "wv": by_head(a["L0_attn_Wv"]),
        "bv": np.ascontiguousarray(np.broadcast_to(a["L0_attn_bv"].reshape(1, -1), (P, NG * D))),
        "router": a["L0_ffn_router_w"], "gate": a["L0_ffn_gate_w"],
        "up": a["L0_ffn_up_w"], "down": a["L0_ffn_down_w"],
        "constf": cf, "constb": cbf.astype(ml_dtypes.bfloat16),
    }
    nc = bacc.Bacc("TRN2", target_bir_lowering=False, num_devices=1)
    args = [nc.dram_tensor(n, v.shape, mybir.dt.from_np(v.dtype), kind="ExternalInput").ap()
            for n, v in arrays.items()]
    out = nc.dram_tensor("out", (T, H), F32, kind="ExternalOutput").ap()
    macaron(nc, *args, out)
    r = run_bass_kernel_spmd(nc, [arrays], core_ids=[0])
    return r.results[0]["out"].reshape(B, S, H)
```

```python
from contextlib import ExitStack, nullcontext

import concourse.bass as bass
import numpy as np
from concourse import mybir

F32 = mybir.dt.float32
BF16 = mybir.dt.bfloat16
I32 = mybir.dt.int32
ALU = mybir.AluOpType
ACT = mybir.ActivationFunctionType
AX = mybir.AxisListType

P = 128
B, S, H = 8, 256, 256
T = B * S
NT = T // P
C = H // P
TB = S // P
NE, I = 8, 512
IC = I // P
NS = NT + NE - 1
WE = 3 * C * I
NH, NG, D = 16, 4, 16
HG = NH // NG
PAD = 2 * T
EPS = 1e-5
RSQRT_MAGIC = float(0x5F3759DF)
NEG = -1e30
Q_PART = (0, 0, 0, 2, 1, 1)
K_PART = (2, 1, 0, 0, 0, 1)
KROWS = len(Q_PART) * D
XG, OB, QB, VB = 4, 4, 3, 4

CONST = {"ident": P, "c128": NS + 1, "desc": NE, "lower": NE * NE, "jrow": NS, "toks": NT * 2}
CONST_AT = dict(zip(CONST, np.cumsum([0] + list(CONST.values())[:-1]).tolist()))
CONST_N = sum(CONST.values())
CONSTB = {"identb": P, "before": P, "ones": P, "iota": P, "mask": HG * P}
CONSTB_AT = dict(zip(CONSTB, np.cumsum([0] + list(CONSTB.values())[:-1]).tolist()))
CONSTB_N = sum(CONSTB.values())


def blocks_of(parts, part):
    at = [k for k, p in enumerate(parts) if p == part]
    step = at[1] - at[0] if len(at) > 1 else 1
    assert at == list(range(at[0], at[-1] + 1, step))
    return slice(at[0], at[-1] + 1, step)


def constants():
    p = np.arange(P)
    f = np.zeros((P, CONST_N), np.float32)
    b = np.zeros((P, CONSTB_N), np.float32)

    def put(a, at, name, v):
        v = np.asarray(v, np.float32).reshape(-1, np.asarray(v).shape[-1])
        a[:, at[name]:at[name] + v.shape[1]] = v

    put(f, CONST_AT, "ident", np.eye(P))
    put(f, CONST_AT, "c128", np.arange(NS + 1)[None] * P)
    put(f, CONST_AT, "desc", NE - np.arange(NE)[None])
    put(f, CONST_AT, "lower", (np.arange(NE)[None, :] < np.arange(NE)[:, None]).reshape(1, -1))
    put(f, CONST_AT, "jrow", np.arange(NS)[None])
    toks = np.zeros((P, NT, 2))
    toks[:, :, 0] = P * np.arange(NT)[None] - PAD
    toks[:, :, 1] = p[:, None]
    put(f, CONST_AT, "toks", toks.reshape(P, -1))
    put(b, CONSTB_AT, "identb", np.eye(P))
    put(b, CONSTB_AT, "before", p[:, None] < p[None, :])
    put(b, CONSTB_AT, "ones", np.ones((1, P)))
    put(b, CONSTB_AT, "iota", p[None, :])
    put(b, CONSTB_AT, "mask", np.tile(np.where(p[None, :] > p[:, None], NEG, 0.0), (1, HG)))
    return f, b


def macaron(nc, x, wq, bq, wk, bk, wv, bv, router, gate, up, down, constf, constb, zrow,
            out):
    with ExitStack() as ctx:
        def sb(name, shape, dt=F32):
            return ctx.enter_context(nc.sbuf_tensor(name, shape, dt))

        def sem(name):
            return ctx.enter_context(nc.semaphore(name))

        def dram(name, shape, dt=F32):
            return nc.dram_tensor(name, shape, dt).ap()

        rows = [dram(f"rows{l}", (T, 2 * H)) for l in range(2)]
        x2d = dram("x2d", (T, H))
        qd = dram("qd", (QB, len(Q_PART), D * NH * S), BF16)
        kd = dram("kd", (QB, len(K_PART), D * NG * S), BF16)
        md = dram("md", (QB, NH, S), BF16)
        ffn_out = [x2d, out]

        W = sb("W", [P, NE * WE])
        xt = sb("xt", [P, NT, H])
        xn = sb("xn", [P, 2, TB, H])
        xnT = sb("xnT", [P, 2, C, S])
        xnr = sb("xnr", [P, TB, H])
        xnrT = sb("xnrT", [P, C, S])
        wr = sb("wr", [P, C, NE])
        wq_s = sb("wq_s", [P, C, NH * D])
        wk_s = sb("wk_s", [P, C, NG * D])
        wv_s = sb("wv_s", [P, C, NG * D])
        bq_s = sb("bq_s", [P, 2])
        bk_s = sb("bk_s", [NG * D, 1])
        bv_s = sb("bv_s", [P, NG * D])
        cf = sb("cf", [P, CONST_N])
        cb = sb("cb", [P, CONSTB_N], BF16)
        bn = sb("bn", [P, NT, 6])
        mv = sb("mv", [P, NT, 2])
        ve = sb("ve", [P, NT])
        hv = sb("hv", [P, NT], I32)
        rs = sb("rs", [P, NT], I32)
        nw = sb("nw", [P, NT])
        lg = sb("lg", [P, NT, NE])
        sg = sb("sg", [P, NT, NE])
        mx = sb("mx", [P, NT])
        eq = sb("eq", [P, NT, NE])
        pm = sb("pm", [P, NT])
        oh = sb("oh", [P, NT, NE], BF16)
        tot = sb("tot", [P, NE])
        tgt = sb("tgt", [P, NE, NT])
        ntl = sb("ntl", [P, NE])
        lw = sb("lw", [P, NE, NE])
        bt = sb("bt", [P, 3, NE])
        rk = sb("rk", [P, NT, NE])
        pos = sb("pos", [P, NT])
        eg = sb("eg", [1, NS, NE])
        ef = sb("ef", [1, 2, NS])
        eoff = sb("eoff", [1, NS + 1], I32)
        gj = sb("gj", [P, NT, NS + 1])
        jt = sb("jt", [P, 2, NT])
        rb = sb("rb", [P, NT], BF16)
        J = sb("J", [P, NT, NS])
        vals = sb("vals", [P, NT, 5])
        mh = sb("mh", [P, NT, 2], BF16)
        mr = sb("mr", [P, NT])
        R1 = sb("R1", [P, NT, P], BF16)
        J5 = sb("J5", [P, NT, 5, NS], BF16)
        sl = sb("sl", [P, 5, NS])
        tf = sb("tf", [P, 2, NS])
        sidx = sb("sidx", [P, NS], I32)
        gidx = sb("gidx", [P, NS], I32)
        mp2 = sb("mp2", [P, 2, NS])
        area = sb("area", [P, QB * (NH + NG) * S // 2])
        xn0 = area[:, 0:NT * H].rearrange("p (t f) -> p t f", t=NT)

        def part(at, *shape):
            n = int(np.prod(shape))
            names = "abc"[:len(shape)]
            v = area[:, at:at + n]
            if len(shape) > 1:
                v = v.rearrange(f"p ({' '.join(names)}) -> p {' '.join(names)}",
                                **dict(zip(names, shape)))
            return v, at + n

        xg, used = part(0, XG, 2 * H)
        xT, used = part(used, 2, C, P)
        sil, used = part(used, 2, I)
        hh, used = part(used, 2, I)
        hT, used = part(used, 2, IC, P)
        ob, used = part(used, OB, H)
        q32 = sb("q32", [P, 2, S])
        qr = sb("qr", [P, 2, S])
        qp = sb("qp", [P, 3, 2, S], BF16)
        k32 = sb("k32", [NG * D, S])
        kr = sb("kr", [NG * D, S])
        kp = sb("kp", [NG * D, 3, S], BF16)
        half = QB * NH * S // 2
        Qs = area[:, 0:half].bitcast(BF16).rearrange("p (r h s) -> p r h s", r=QB, h=NH)
        Ks = area[:, half:].bitcast(BF16).rearrange("p (r h s) -> p r h s", r=QB, h=NG)
        V = sb("V", [P, VB, TB, NG, 2 * D])
        mxa = sb("mxa", [P, 2, TB, NH])
        nmx = sb("nmx", [P, TB, NH], BF16)
        mT = sb("mT", [NH, S], BF16)
        fin = sb("fin", [1, 2])
        PT = sb("PT", [P, 2, 3 * 512])
        OT = sb("OT", [P, 2, S])
        rc = sb("rc", [P, TB, HG])
        at = sb("at", [P, TB, HG * D])

        bank = [ctx.enter_context(nc.psum_tensor(f"bank{i}", [P, 512], F32)) for i in range(8)]
        bankm = bank[6][:, 0:P].bitcast(BF16)

        def cst(name):
            return cf[:, CONST_AT[name]:CONST_AT[name] + CONST[name]]

        def cstb(name):
            return cb[:, CONSTB_AT[name]:CONSTB_AT[name] + CONSTB[name]]

        ident, identb = cst("ident"), cstb("identb")
        rsf = rs[:].bitcast(F32)

        s_x = [sem(f"s_x{b}") for b in range(B)]
        s_cst = sem("s_cst")
        s_w = sem("s_w")
        s_x2 = [sem(f"s_x2_{b}") for b in range(B)]
        s_const = sem("s_const")
        dve = sem("dve")
        pool = sem("pool")
        s_st = [sem(f"s_st{k}") for k in range(3)]
        s_rs = [sem(f"s_rs{k}") for k in range(3)]
        s_xn = [sem(f"s_xn{k}") for k in range(3)]
        s_xp = [sem(f"s_xp{k}") for k in range(3)]
        s_xs = [sem(f"s_xs{k}") for k in range(3)]
        s_row = [sem(f"s_row{l}") for l in range(2)]
        s_lp = [sem(f"s_lp{l}") for l in range(2)]
        s_ls = [sem(f"s_ls{l}") for l in range(2)]
        s_ex = [sem(f"s_ex{l}") for l in range(2)]
        s_oh = [sem(f"s_oh{l}") for l in range(2)]
        s_rk = [sem(f"s_rk{l}") for l in range(2)]
        s_rj = [sem(f"s_rj{l}") for l in range(2)]
        s_sl = [sem(f"s_sl{l}") for l in range(2)]
        s_ix = [sem(f"s_ix{l}") for l in range(2)]
        f_g = [[sem(f"f_g{l}_{i}") for i in range(XG)] for l in range(2)]
        f_s = [[sem(f"f_s{l}_{i}") for i in range(OB)] for l in range(2)]
        f_xp = [sem(f"f_xp{l}") for l in range(2)]
        f_xs = [sem(f"f_xs{l}") for l in range(2)]
        f_gp = [sem(f"f_gp{l}") for l in range(2)]
        f_up = [sem(f"f_up{l}") for l in range(2)]
        f_si = [sem(f"f_si{l}") for l in range(2)]
        f_h = [sem(f"f_h{l}") for l in range(2)]
        f_hp = [sem(f"f_hp{l}") for l in range(2)]
        f_hs = [sem(f"f_hs{l}") for l in range(2)]
        f_y = [sem(f"f_y{l}") for l in range(2)]
        f_o = [sem(f"f_o{l}") for l in range(2)]
        a_q = sem("a_q")
        a_kv = sem("a_kv")
        a_q32 = sem("a_q32")
        a_k32 = sem("a_k32")
        a_v = sem("a_v")
        a_qh = sem("a_qh")
        a_qr = sem("a_qr")
        a_qm = sem("a_qm")
        a_ql = sem("a_ql")
        a_qd = sem("a_qd")
        a_qs = [sem(f"a_qs{i}") for i in range(QB)]
        a_a = sem("a_a")
        a_am = sem("a_am")
        a_nm = sem("a_nm")
        a_mp = sem("a_mp")
        a_md = sem("a_md")
        a_ms = sem("a_ms")
        a_mq = [sem(f"a_mq{i}") for i in range(QB)]
        a_st = sem("a_st")
        a_e = sem("a_e")
        a_pm = sem("a_pm")
        a_o = sem("a_o")
        a_os = sem("a_os")
        a_ot = sem("a_ot")
        a_x3 = sem("a_x3")
        s_fin = [sem(f"s_fin{l}") for l in range(2)]

        block = ctx.enter_context(nc.Block())

        def tiles(k, b):
            return (b * NT // 2, (b + 1) * NT // 2) if k == 0 else (TB * b, TB * b + TB)

        def ln_stats(k, b, seen):
            t0, t1 = tiles(k, b)
            for t in range(t0, t1):
                if k == 0 and t % TB == 0:
                    nc.vector.wait_ge(s_x[t // TB], 16)
                nc.vector.bn_stats(bn[:, t, :], xt[:, t, :]).then_inc(dve, 1)
            seen[0] += t1 - t0
            nc.vector.wait_ge(dve, seen[0])
            for t in range(t0, t1):
                nc.vector.bn_aggr(mv[:, t, :], bn[:, t, :]).then_inc(dve, 1)
            seen[0] += t1 - t0
            nc.vector.wait_ge(dve, seen[0])
            link(nc.vector.tensor_scalar(ve[:, t0:t1], mv[:, t0:t1, 1], EPS, None, ALU.add), seen)
            link(nc.vector.tensor_scalar(hv[:, t0:t1], ve[:, t0:t1].bitcast(I32), 1, None,
                                         ALU.arith_shift_right), seen)
            nc.vector.tensor_scalar(rs[:, t0:t1], hv[:, t0:t1], -1.0, RSQRT_MAGIC,
                                    ALU.mult, ALU.add).then_inc(s_st[k], 1)

        def link(ins, seen):
            seen[0] += 1
            ins.then_inc(dve, 1)
            nc.vector.wait_ge(dve, seen[0])

        def mark(ins, seen):
            seen[0] += 1
            ins.then_inc(dve, 1)

        def plink(ins, seen):
            seen[0] += 1
            ins.then_inc(pool, 1)
            nc.gpsimd.wait_ge(pool, seen[0])

        def newton(v, r, n, done, seen):
            for step in range(3):
                plink(nc.gpsimd.tensor_tensor(n, r, r, ALU.mult), seen)
                plink(nc.gpsimd.tensor_tensor(n, n, v, ALU.mult), seen)
                plink(nc.gpsimd.tensor_scalar(n, n, -0.5, 1.5, ALU.mult, ALU.add), seen)
                last = nc.gpsimd.tensor_tensor(r, r, n, ALU.mult)
                if step < 2:
                    plink(last, seen)
            last.then_inc(done, 1)

        def ln_newton(k, b, seen):
            t0, t1 = tiles(k, b)
            nc.gpsimd.wait_ge(s_st[k], b + 1)
            newton(ve[:, t0:t1], rsf[:, t0:t1], nw[:, t0:t1], s_rs[k], seen)

        def of_round(a, b):
            a = a.rearrange("p (b t) -> p b t", t=TB)
            lo, hi = max(b - 1, 0), b + 5
            if b == 0:
                return a[:, hi:hi + 1]
            return a[:, lo:hi + 1:hi - lo] if hi < B else a[:, lo:lo + 1]

        def round_tiles(b):
            return ([TB * (b - 1) + i for i in range(TB)] if b >= 1 else []) + \
                   ([TB * (b + 5) + i for i in range(TB)] if b + 5 < B else [])

        def round_stats(b, seen):
            if b >= 1:
                nc.vector.wait_ge(a_x3, NG * b)
            if b + 5 < B:
                nc.vector.wait_ge(s_x2[b + 5], 16)
            for t in round_tiles(b):
                mark(nc.vector.bn_stats(bn[:, t, :], xt[:, t, :]), seen)

        def round_aggr(b, seen):
            nc.vector.wait_ge(dve, seen[0])
            for t in round_tiles(b):
                mark(nc.vector.bn_aggr(mv[:, t, :], bn[:, t, :]), seen)

        def round_eps(b, seen):
            nc.vector.wait_ge(dve, seen[0])
            mark(nc.vector.tensor_scalar(of_round(ve[:], b), of_round(mv[:, :, 1], b), EPS, None, ALU.add), seen)

        def round_half(b, seen):
            nc.vector.wait_ge(dve, seen[0])
            mark(nc.vector.tensor_scalar(of_round(hv[:], b), of_round(ve[:].bitcast(I32), b), 1, None,
                                         ALU.arith_shift_right), seen)

        def round_guess(b, seen):
            nc.vector.wait_ge(dve, seen[0])
            nc.vector.tensor_scalar(of_round(rs[:], b), of_round(hv[:], b), -1.0, RSQRT_MAGIC,
                                    ALU.mult, ALU.add).then_inc(s_st[2], 1)

        def round_newton(b, seen):
            nc.gpsimd.wait_ge(s_st[2], b + 1)
            newton(of_round(ve[:], b), of_round(rsf, b), of_round(nw[:], b), s_rs[2], seen)

        def ln_apply(k, b):
            done, n = ((s_rs[0], 2 * b // B + 1), (s_rs[1], b + 1) if b < 5 else (s_rs[2], b - 4),
                       (s_rs[2], b + 2))[k]
            nc.vector.wait_ge(done, n)
            dst = (xn0[:, TB * b:TB * b + TB], xn[:, b % 2], xnr[:])[k]
            if k == 1 and b >= 2:
                nc.vector.wait_ge(s_xp[k], b - 1)
            if k == 2 and b >= 1:
                nc.vector.wait_ge(s_row[1], 32 * b)
                nc.vector.wait_ge(s_xp[k], b)
            for i in range(TB):
                t = TB * b + i
                nc.vector.tensor_scalar(dst[:, i, :], xt[:, t, :], mv[:, t, 0:1], rsf[:, t:t + 1],
                                        ALU.subtract, ALU.mult).then_inc(s_xn[k], 1)

        def ln_transpose(k, b, ps):
            src = (xn0[:, TB * b:TB * b + TB], xn[:, b % 2], xnr[:])[k]
            nc.tensor.wait_ge(s_xn[k], TB * (b + 1))
            o = ps[:].rearrange("p (c s) -> p c s", c=C)
            for i in range(TB):
                for c in range(C):
                    last = nc.tensor.transpose(o[:, c, i * P:(i + 1) * P],
                                               src[:, i, c * P:(c + 1) * P], ident)
            last.then_inc(s_xp[k], 1)

        def ln_evacuate(k, b, ps):
            nc.scalar.wait_ge(s_xp[k], b + 1)
            dst = xnT[:, b % 2] if k < 2 else xnrT[:]
            nc.scalar.copy(dst, ps[:].rearrange("p (c s) -> p c s", c=C)).then_inc(s_xs[k], 1)

        def logits(l, b, ps):
            k = 2 * l
            src = xnT[:, b % 2] if k < 2 else xnrT[:]
            nc.tensor.wait_ge(s_xs[k], b + 1)
            for i in range(TB):
                for c in range(C):
                    last = nc.tensor.matmul(ps[:, i * NE:(i + 1) * NE], src[:, c, i * P:(i + 1) * P],
                                            wr[:, c, :], start=(c == 0), stop=(c == C - 1))
            last.then_inc(s_lp[l], 1)

        def logits_copy(l, b, ps):
            nc.vector.wait_ge(s_lp[l], b + 1)
            nc.vector.tensor_copy(lg[:, TB * b:TB * b + TB, :],
                                  ps[:, 0:TB * NE].rearrange("p (t e) -> p t e", e=NE)).then_inc(s_ls[l], 1)

        def rows_written(eng, l):
            eng.wait_ge(s_row[l], 32 * B)

        def write_rows(eng, l, b):
            k = 2 * l
            src = (xn0[:, TB * b:TB * b + TB], xn[:, b % 2], xnr[:])[k]
            dst = rows[l][S * b:S * b + S, :].rearrange("(t p) f -> p t f", p=P)
            eng.wait_ge(s_xn[k], TB * (b + 1))
            eng.dma_start(dst[:, :, 0:H], xt[:, TB * b:TB * b + TB, :]).then_inc(s_row[l], 16)
            eng.dma_start(dst[:, :, H:2 * H], src).then_inc(s_row[l], 16)

        def route_dve(l, seen):
            v = nc.vector
            v.wait_ge(s_ex[l], 1)
            link(v.tensor_scalar(sg[:], sg[:], 1.0, None, ALU.add), seen)
            link(v.reciprocal(sg[:], sg[:]), seen)
            link(v.tensor_reduce(mx[:], sg[:], AX.X, ALU.max), seen)
            link(v.tensor_tensor(eq[:], sg[:], mx[:].unsqueeze(2).to_broadcast([P, NT, NE]), ALU.is_equal), seen)
            desc = cst("desc").unsqueeze(1).to_broadcast([P, NT, NE])
            link(v.tensor_tensor(eq[:], eq[:], desc, ALU.mult), seen)
            link(v.tensor_reduce(pm[:], eq[:], AX.X, ALU.max), seen)
            v.tensor_tensor(oh[:], desc, pm[:].unsqueeze(2).to_broadcast([P, NT, NE]),
                            ALU.is_equal).then_inc(s_oh[l], 1)
            link(v.tensor_copy(mh[:, :, 0], mx[:]), seen)
            link(v.tensor_tensor(mr[:], mx[:], mh[:, :, 0], ALU.subtract), seen)
            link(v.tensor_copy(mh[:, :, 1], mr[:]), seen)
            v.tensor_copy(vals[:, :, 0:2], cst("toks").rearrange("p (t k) -> p t k", k=2)).then_inc(dve, 1)
            v.tensor_copy(vals[:, :, 2:4], mh[:]).then_inc(dve, 1)
            v.tensor_tensor(vals[:, :, 4], mr[:], mh[:, :, 1], ALU.subtract).then_inc(dve, 1)
            seen[0] += 3
            v.wait_ge(s_rk[l], 1)
            link(v.tensor_copy(tot[:], bank[4][:, P:P + NE]), seen)
            link(v.tensor_tensor(tgt[:], tot[:].unsqueeze(2).to_broadcast([P, NE, NT]),
                                 cst("c128")[:, 0:NT].unsqueeze(1).to_broadcast([P, NE, NT]), ALU.is_gt), seen)
            link(v.tensor_reduce(ntl[:], tgt[:], AX.X, ALU.add), seen)
            link(v.tensor_tensor(lw[:], ntl[:].unsqueeze(1).to_broadcast([P, NE, NE]),
                                 cst("lower").rearrange("p (e f) -> p e f", e=NE), ALU.mult), seen)
            link(v.tensor_reduce(bt[:, 0, :], lw[:], AX.X, ALU.add), seen)
            v.tensor_tensor(bt[:, 1, :], bt[:, 0, :], ntl[:], ALU.add).then_inc(dve, 1)
            seen[0] += 1
            link(v.tensor_scalar(bt[:, 2, :], bt[:, 0, :], float(P), None, ALU.mult), seen)
            link(v.tensor_tensor(rk[:], bank[4][:, 0:P].rearrange("p (t e) -> p t e", e=NE),
                                 bt[:, 2, :].unsqueeze(1).to_broadcast([P, NT, NE]), ALU.add), seen)
            link(v.tensor_tensor(rk[:], rk[:], oh[:], ALU.mult), seen)
            link(v.tensor_reduce(pos[:], rk[:], AX.X, ALU.add), seen)
            link(v.tensor_tensor(gj[:], pos[:].unsqueeze(2).to_broadcast([P, NT, NS + 1]),
                                 cst("c128").unsqueeze(1).to_broadcast([P, NT, NS + 1]), ALU.is_ge), seen)
            v.tensor_tensor(J[:], gj[:, :, 0:NS], gj[:, :, 1:NS + 1], ALU.subtract).then_inc(dve, 1)
            seen[0] += 1
            link(v.tensor_reduce(jt[:, 0, :], gj[:], AX.X, ALU.add), seen)
            link(v.tensor_scalar(jt[:, 1, :], jt[:, 0, :], -float(P), float(P), ALU.mult, ALU.add), seen)
            link(v.tensor_tensor(rb[:], pos[:], jt[:, 1, :], ALU.add), seen)
            h = NT // 2
            for t in (0, h):
                v.tensor_tensor(R1[:, t:t + h, :], cstb("iota").unsqueeze(1).to_broadcast([P, h, P]),
                                rb[:, t:t + h].unsqueeze(2).to_broadcast([P, h, P]),
                                ALU.is_equal).then_inc(s_rj[l], 1)
                v.tensor_tensor(J5[:, t:t + h], J[:, t:t + h, :].unsqueeze(2).to_broadcast([P, h, 5, NS]),
                                vals[:, t:t + h, :].unsqueeze(3).to_broadcast([P, h, 5, NS]),
                                ALU.mult).then_inc(s_rj[l], 1)
            link(v.tensor_tensor(eg[:], bt[0:1, 1, :].unsqueeze(1).to_broadcast([1, NS, NE]),
                                 cst("jrow")[0:1, :].unsqueeze(2).to_broadcast([1, NS, NE]), ALU.is_le), seen)
            link(v.tensor_reduce(ef[:, 0, :], eg[:], AX.X, ALU.add), seen)
            v.tensor_scalar(ef[:, 1, :], ef[:, 0, :], float(NE - 1), float(WE), ALU.min, ALU.mult).then_inc(dve, 1)
            seen[0] += 1
            v.wait_ge(dve, seen[0])
            v.tensor_copy(eoff[:, 0:NS], ef[:, 1, :]).then_inc(s_ix[l], 1)
            v.tensor_copy(eoff[:, NS:NS + 1], bt[0:1, 1, NE - 1:NE]).then_inc(s_ix[l], 1)
            v.wait_ge(s_sl[l], 1)
            link(v.tensor_copy(sl[:], bank[5][:, 0:5 * NS].rearrange("p (k j) -> p k j", k=5)), seen)
            link(v.scalar_tensor_tensor(out=tf[:, 0, :], in0=sl[:, 0, :], scalar=float(PAD), in1=sl[:, 1, :],
                                        op0=ALU.add, op1=ALU.add), seen)
            v.tensor_copy(sidx[:], tf[:, 0, :]).then_inc(s_ix[l], 1)
            v.tensor_scalar(gidx[:], tf[:, 0, :], float(T - 1), None, ALU.min).then_inc(s_ix[l], 1)
            link(v.tensor_tensor(mp2[:, 0, :], sl[:, 2, :], sl[:, 3, :], ALU.add), seen)
            link(v.tensor_tensor(mp2[:, 0, :], mp2[:, 0, :], sl[:, 4, :], ALU.add), seen)
            link(v.tensor_scalar(mp2[:, 1, :], mp2[:, 0, :], 0.5, None, ALU.mult), seen)

        def route_act(l):
            nc.scalar.wait_ge(s_ls[l], B)
            nc.scalar.activation(sg[:], lg[:], ACT.Exp, scale=-1.0).then_inc(s_ex[l], 1)

        def route_pe(l):
            pe = nc.tensor
            pe.wait_ge(s_oh[l], 1)
            o2 = oh[:].rearrange("p t e -> p (t e)")
            pe.matmul(bank[4][:, 0:P], cstb("before"), o2, start=True, stop=False)
            for s in range(1, NT):
                pe.matmul(bank[4][:, s * NE:P], cstb("ones"), o2[:, 0:P - s * NE],
                          start=False, stop=(s == NT - 1))
            for t in range(NT):
                last = pe.matmul(bank[4][:, P:P + NE], cstb("ones"), oh[:, t, :],
                                 start=(t == 0), stop=(t == NT - 1))
            last.then_inc(s_rk[l], 1)
            for t in range(NT):
                if t % (NT // 2) == 0:
                    pe.wait_ge(s_rj[l], 2 if t == 0 else 4)
                last = pe.matmul(bank[5][:, 0:5 * NS], R1[:, t, :],
                                 J5[:, t].rearrange("p k j -> p (k j)"), start=(t == 0), stop=(t == NT - 1))
            last.then_inc(s_sl[l], 1)

        def tiles_used(eng, l):
            eng.wait_ge(s_ix[l], 4)
            return eng.value_load(eoff[0:1, NS:NS + 1], min_val=NT, max_val=NS)

        def if_tile(eng, used, j):
            return nullcontext() if j < NT else eng.If(used > j)

        def gather(l, j, k):
            nc.gpsimd.indirect_dma_start(
                xg[:, k % XG, :], None, rows[l],
                bass.IndirectOffsetOnAxis(ap=gidx[:, bass.ds(j, 1)], axis=0)).then_inc(f_g[l][k % XG], 16)

        def scatter(l, j, k):
            nc.gpsimd.indirect_dma_start(
                ffn_out[l], bass.IndirectOffsetOnAxis(ap=sidx[:, bass.ds(j, 1)], axis=0),
                ob[:, k % OB, :], None, bounds_check=T - 1, oob_is_err=False).then_inc(f_s[l][k % OB], 16)

        def scattered(used, l):
            p = nc.gpsimd
            for j in range(NT - OB, NS):
                with if_tile(p, used, j):
                    p.wait_ge(f_s[l][j % OB], 16 * (j // OB + 1))
                    p.nop()
            nc.gpsimd.memset(fin[:], 0.0).then_inc(s_fin[l], 1)

        def ffn_pool(l):
            p = nc.gpsimd
            rows_written(p, l)
            used = tiles_used(p, l)
            for j in range(XG):
                gather(l, j, j)
            for j in range(1, NS + 1):
                with if_tile(p, used, j - 1):
                    p.wait_ge(f_o[l], j)
                    scatter(l, j - 1, j - 1)
                if j + XG - 1 < NS:
                    with if_tile(p, used, j + XG - 1):
                        gather(l, j + XG - 1, j + XG - 1)
            scattered(used, l)

        def weights_at(j):
            return nc.tensor.value_load(eoff[0:1, bass.ds(j, 1)], min_val=0, max_val=(NE - 1) * WE)

        def ffn_pe_step(l, j, k, offs, used):
            pe = nc.tensor
            if 1 <= j:
                with if_tile(pe, used, j - 1):
                    pe.wait_ge(f_h[l], j)
                    if j >= 2:
                        pe.wait_ge(f_hs[l], j - 1)
                    for i in range(IC):
                        last = pe.transpose(bank[4][:, i * P:(i + 1) * P],
                                            hh[:, (k - 1) % 2, i * P:(i + 1) * P], ident)
                    last.then_inc(f_hp[l], 1)
            for n in ([0, 1] if j == 0 else [j + 1]):
                if n < NS:
                    with if_tile(pe, used, n):
                        pe.wait_ge(f_g[l][n % XG], 16 * (n // XG + 1))
                        if n >= 1:
                            pe.wait_ge(f_xs[l], n)
                        for c in range(C):
                            last = pe.transpose(bank[5][:, c * P:(c + 1) * P],
                                                xg[:, n % XG, H + c * P:H + (c + 1) * P], ident)
                        last.then_inc(f_xp[l], 1)
            if j < NS:
                with if_tile(pe, used, j):
                    pe.wait_ge(f_xs[l], j + 1)
                    if j >= 2:
                        pe.wait_ge(f_si[l], j - 1)
                        pe.wait_ge(f_h[l], j - 1)
                    for m, done in ((0, f_gp), (1, f_up)):
                        for c in range(C):
                            last = pe.matmul(bank[2 * m + k % 2][:], xT[:, k % 2, c, :],
                                             W[:, bass.ds(offs[j] + (m * C + c) * I, I)],
                                             start=(c == 0), stop=(c == C - 1))
                        last.then_inc(done[l], 1)
                if j + 1 < NS:
                    offs[j + 1] = weights_at(j + 1)
            if j >= 1:
                with if_tile(pe, used, j - 1):
                    pe.wait_ge(f_hs[l], j)
                    if j >= 3:
                        pe.wait_ge(f_o[l], j - 2)
                    for i in range(IC):
                        last = pe.matmul(bank[6 + (k - 1) % 2][:, 0:H], hT[:, (k - 1) % 2, i, :],
                                         W[:, bass.ds(offs[j - 1] + 2 * C * I + i * H, H)],
                                         start=(i == 0), stop=(i == IC - 1))
                    last.then_inc(f_y[l], 1)

        def ffn_act_step(l, j, k, used):
            a = nc.scalar
            if j >= 1:
                with if_tile(a, used, j - 1):
                    a.wait_ge(f_hp[l], j)
                    if j >= 3:
                        a.wait_ge(f_y[l], j - 2)
                    a.copy(hT[:, (k - 1) % 2], bank[4][:].rearrange("p (i s) -> p i s", i=IC)).then_inc(f_hs[l], 1)
            if j < NS:
                with if_tile(a, used, j):
                    a.wait_ge(f_gp[l], j + 1)
                    if j >= 2:
                        a.wait_ge(f_h[l], j - 1)
                    a.activation(sil[:, k % 2, :], bank[k % 2][:], ACT.Silu).then_inc(f_si[l], 1)

        def ffn_dve_step(l, j, k, used):
            v = nc.vector
            for n in ([0, 1] if j == 0 else [j + 1]):
                if n < NS:
                    with if_tile(v, used, n):
                        v.wait_ge(f_xp[l], n + 1)
                        if n >= 2:
                            v.wait_ge(f_up[l], n - 1)
                        v.tensor_copy(xT[:, n % 2], bank[5][:, 0:H].rearrange("p (c s) -> p c s", c=C)).then_inc(f_xs[l], 1)
            if j < NS:
                with if_tile(v, used, j):
                    v.wait_ge(f_si[l], j + 1)
                    v.wait_ge(f_up[l], j + 1)
                    if j >= 2:
                        v.wait_ge(f_hp[l], j - 1)
                    v.tensor_tensor(hh[:, k % 2, :], sil[:, k % 2, :], bank[2 + k % 2][:], ALU.mult).then_inc(f_h[l], 1)
            if j >= 1:
                with if_tile(v, used, j - 1):
                    v.wait_ge(f_y[l], j)
                    if j > OB:
                        v.wait_ge(f_s[l][(j - 1) % OB], 16 * ((j - 1) // OB))
                    v.scalar_tensor_tensor(out=ob[:, (k - 1) % OB, :], in0=bank[6 + (k - 1) % 2][:, 0:H],
                                           scalar=mp2[:, 1, bass.ds(j - 1, 1)], in1=xg[:, (k - 1) % XG, 0:H],
                                           op0=ALU.mult, op1=ALU.add).then_inc(f_o[l], 1)

        def a_proj_q(b):
            pe = nc.tensor
            pe.wait_ge(s_xs[1], b + 1)
            for m in range(2):
                for c in range(C):
                    last = pe.matmul(bank[7][:, m * S:(m + 1) * S], wq_s[:, c, m * P:(m + 1) * P],
                                     xnT[:, b % 2, c, :], start=(c == 0), stop=(c == C - 1))
            last.then_inc(a_q, 1)

        def a_proj_kv(b):
            pe = nc.tensor
            for c in range(C):
                pe.matmul(bank[6][0:NG * D, 0:S], wk_s[:, c, :], xnT[:, b % 2, c, :],
                          start=(c == 0), stop=(c == C - 1))
            for i in range(TB):
                for c in range(C):
                    last = pe.matmul(bank[6][:, S + i * NG * D:S + (i + 1) * NG * D],
                                     xnT[:, b % 2, c, i * P:(i + 1) * P], wv_s[:, c, :],
                                     start=(c == 0), stop=(c == C - 1))
            last.then_inc(a_kv, 1)

        def a_split_act(b):
            a = nc.scalar
            a.wait_ge(a_q, b + 1)
            if b >= 1:
                a.wait_ge(a_qr, 2 * b)
            for m in range(2):
                last = a.activation(q32[:, m, :], bank[7][:, m * S:(m + 1) * S], ACT.Identity,
                                    bias=bq_s[:, m:m + 1])
            last.then_inc(a_q32, 1)

        def a_split_act2(b):
            a = nc.scalar
            a.wait_ge(a_q32, b + 1)
            a.wait_ge(a_k32, b + 1)
            if b >= 1:
                a.wait_ge(a_qd, 96 * b)
            a.copy(qp[:, 0], q32[:])
            a.copy(kp[:, 0], k32[:]).then_inc(a_qh, 1)

        def a_split_act3(b):
            a = nc.scalar
            a.wait_ge(a_qr, 2 * b + 2)
            a.copy(qp[:, 1], qr[:])
            a.copy(kp[:, 1], kr[:]).then_inc(a_qm, 1)

        def a_split_dve(b):
            v = nc.vector
            v.wait_ge(a_kv, b + 1)
            v.tensor_scalar(k32[:], bank[6][0:NG * D, 0:S], bk_s[:], None, ALU.add).then_inc(a_k32, 1)
            v.tensor_tensor(V[:, b % VB, :, :, 0:D],
                            bank[6][:, S:S + TB * NG * D].rearrange("p (t g d) -> p t g d", t=TB, g=NG),
                            bv_s[:].rearrange("p (g d) -> p g d", g=NG).unsqueeze(1).to_broadcast([P, TB, NG, D]),
                            ALU.add).then_inc(a_v, 1)

        def a_split_dve2(b):
            v = nc.vector
            v.wait_ge(a_qh, b + 1)
            v.tensor_tensor(qr[:], q32[:], qp[:, 0], ALU.subtract).then_inc(a_qr, 1)
            v.tensor_tensor(kr[:], k32[:], kp[:, 0], ALU.subtract).then_inc(a_qr, 1)

        def a_split_dve3(b):
            v = nc.vector
            v.wait_ge(a_qm, b + 1)
            v.tensor_tensor(qp[:, 2], qr[:], qp[:, 1], ALU.subtract).then_inc(a_ql, 1)
            v.tensor_tensor(kp[:, 2], kr[:], kp[:, 1], ALU.subtract).then_inc(a_ql, 1)

        def a_stack(sp, b):
            r = b % QB
            for part in range(3):
                sp.wait_ge((a_qh, a_qm, a_ql)[part], (1, 1, 2)[part] * (b + 1))
                k = blocks_of(Q_PART, part)
                n = Q_PART.count(part)
                sp.dma_start(qd[r, k].rearrange("k (p f) -> p k f", p=P),
                             qp[:, part].rearrange("p m s -> p (m s)").unsqueeze(1)
                             .to_broadcast([P, n, 2 * S])).then_inc(a_qd, 16)
                k = blocks_of(K_PART, part)
                n = K_PART.count(part)
                sp.dma_start(kd[r, k].rearrange("k (p f) -> p k f", p=NG * D),
                             kp[:, part].unsqueeze(1).to_broadcast([NG * D, n, S])).then_inc(a_qd, 16)

        def a_stack_back(sp, b):
            r = b % QB
            sp.wait_ge(a_qd, 96 * (b + 1))
            if b >= QB:
                sp.wait_ge(a_st, 3 * NG * (b - QB + 1))
                sp.dma_start(Qs[KROWS:KROWS + 1, r], zrow.rearrange("o (h s) -> o h s", h=NH)).then_inc(a_qs[r], 16)
            sp.dma_start(Qs[0:KROWS, r], qd[r].rearrange("k (d h s) -> (k d) h s", d=D, h=NH)).then_inc(a_qs[r], 16)
            sp.dma_start(Ks[0:KROWS, r], kd[r].rearrange("k (d h s) -> (k d) h s", d=D, h=NG)).then_inc(a_qs[r], 16)

        def a_max_row(sp, b):
            r = b % QB
            sp.wait_ge(a_ms, b + 1)
            sp.dma_start(md[r], mT[:]).then_inc(a_md, 16)
            sp.wait_ge(a_md, 16 * (b + 1))
            sp.dma_start(Qs[KROWS:KROWS + 1, r], md[r:r + 1]).then_inc(a_mq[r], 16)

        def a_max_pe(m, u):
            pe = nc.tensor
            b, g = divmod(m, NG)
            r = b % QB
            if g == 0 and u == 0:
                pe.wait_ge(a_qs[r], 48 * (b // QB + 1) - 16)
            n = 3 * m + u
            if n >= 2:
                pe.wait_ge(a_am, n - 1)
            o = bank[3 + n % 2]
            if u == 0:
                for h in range(HG):
                    pe.matmul(o[:, h * P:(h + 1) * P], Qs[:, r, HG * g + h, 0:P],
                              Ks[:, r, g, 0:P], start=(h == 0), stop=False)
                last = pe.matmul(o[:], identb, cstb("mask"), start=False, stop=True)
            else:
                for h in range(2):
                    pe.matmul(o[:, h * S:(h + 1) * S], Qs[:, r, HG * g + 2 * (u - 1) + h, P:S],
                              Ks[:, r, g, :], start=(h == 0), stop=False)
                last = pe.matmul(o[:].rearrange("p (h k) -> p h k", h=2)[:, :, P:S], identb,
                                 cstb("mask")[:, 0:2 * P].rearrange("p (h k) -> p h k", h=2),
                                 start=False, stop=True)
            last.then_inc(a_a, 1)

        def a_max_dve(m, u):
            v = nc.vector
            b, g = divmod(m, NG)
            n = 3 * m + u
            v.wait_ge(a_a, n + 1)
            o = bank[3 + n % 2]
            if u == 0:
                v.tensor_reduce(mxa[:, b % 2, 0, HG * g:HG * g + HG],
                                o[:].rearrange("p (h k) -> p h k", h=HG), AX.X, ALU.max).then_inc(a_am, 1)
            else:
                h0 = HG * g + 2 * (u - 1)
                v.tensor_reduce(mxa[:, b % 2, 1, h0:h0 + 2],
                                o[:].rearrange("p (h k) -> p h k", h=2), AX.X, ALU.max).then_inc(a_am, 1)

        def a_neg_dve(b):
            v = nc.vector
            v.wait_ge(a_am, 3 * NG * (b + 1))
            if b >= 1:
                v.wait_ge(a_mp, b)
            v.tensor_scalar(nmx[:], mxa[:, b % 2], -1.0, None, ALU.mult).then_inc(a_nm, 1)

        def a_neg_pe(b):
            pe = nc.tensor
            pe.wait_ge(a_nm, b + 1)
            for i in range(TB):
                last = pe.transpose(bankm[0:NH, i * P:(i + 1) * P], nmx[:, i, :], identb)
            last.then_inc(a_mp, 1)

        def a_neg_copy(b):
            v = nc.vector
            v.wait_ge(a_mp, b + 1)
            if b >= 1:
                v.wait_ge(a_md, 16 * b)
            v.tensor_copy(mT[:], bankm[0:NH, 0:S]).then_inc(a_ms, 1)

        def a_scores(n, u):
            pe = nc.tensor
            b, g = divmod(n, NG)
            r = b % QB
            if g == 0 and u == 0:
                pe.wait_ge(a_mq[r], 16 * (b // QB + 1))
            if n >= 1:
                pe.wait_ge(a_e, 3 * (n - 1) + u + 1)
            if u < 2:
                rhs = Qs[:, r, HG * g + 2 * u:HG * g + 2 * u + 2, :]
                o = bank[u][:].rearrange("p (h q) -> p h q", h=2)
                k0 = 0
            else:
                rhs = Qs[:, r, HG * g:HG * g + HG, P:S]
                o = bank[u][:].rearrange("p (h q) -> p h q", h=HG)
                k0 = P
            pe.matmul(o, Ks[:, r, g, k0:k0 + P], rhs, start=True, stop=True).then_inc(a_st, 1)

        def a_exp(n, u):
            a = nc.scalar
            a.wait_ge(a_st, 3 * n + u + 1)
            if u == 0 and n >= 2:
                a.wait_ge(a_o, n - 1)
            a.activation(PT[:, n % 2, u * 512:(u + 1) * 512], bank[u][:], ACT.Exp,
                         scale=D ** -0.5).then_inc(a_e, 1)

        def a_mask(n):
            p = nc.gpsimd
            for u, src in ((2, PT[:, n % 2, 0:1024].rearrange("p (h q) -> p h q", h=HG)[:, :, 0:P]),
                           (3, PT[:, n % 2, 1024:1536].rearrange("p (h q) -> p h q", h=HG))):
                p.wait_ge(a_e, 3 * n + u)
                p.affine_select(out=src, in_=src, compare_op=ALU.is_ge, fill=0.0, base=0,
                                pattern=[[0, HG], [1, P]], channel_multiplier=-1).then_inc(a_pm, 1)

        def a_values(n):
            pe = nc.tensor
            b, g = divmod(n, NG)
            pe.wait_ge(a_pm, 2 * n + 2)
            pe.wait_ge(a_v, b + 1)
            if n >= 1:
                pe.wait_ge(a_os, n)
            c0 = (n % 2) * S
            for h in range(HG):
                pe.matmul(bank[5][32 * h:32 * h + 32, c0:c0 + S], V[:, b % VB, 0, g, :],
                          PT[:, n % 2, h * S:(h + 1) * S], start=True, stop=False, tile_position=(0, 32 * h))
            for h in range(HG):
                last = pe.matmul(bank[5][32 * h:32 * h + 32, c0 + P:c0 + S], V[:, b % VB, 1, g, :],
                                 PT[:, n % 2, 1024 + h * P:1024 + (h + 1) * P], start=False, stop=True,
                                 tile_position=(0, 32 * h))
            last.then_inc(a_o, 1)

        def a_values_copy(n):
            a = nc.scalar
            a.wait_ge(a_o, n + 1)
            if n >= 2:
                a.wait_ge(a_ot, n - 1)
            a.copy(OT[:, n % 2, :], bank[5][:, (n % 2) * S:(n % 2) * S + S]).then_inc(a_os, 1)

        def a_heads_pe(n):
            pe = nc.tensor
            pe.wait_ge(a_os, n + 1)
            if n >= 1:
                pe.wait_ge(a_x3, n)
            for i in range(TB):
                last = pe.transpose(bank[7][:, i * P:(i + 1) * P], OT[:, n % 2, i * P:(i + 1) * P], ident)
            last.then_inc(a_ot, 1)

        heads = bank[7][:, 0:S].rearrange("p (t h d) -> p t h d", t=TB, h=HG)

        def a_heads_sum(n, seen):
            nc.vector.wait_ge(a_ot, n + 1)
            mark(nc.vector.reciprocal(rc[:], heads[:, :, :, D]), seen)

        def a_heads_div(n, seen):
            nc.vector.wait_ge(dve, seen[0])
            mark(nc.vector.tensor_tensor(at[:].rearrange("p t (h d) -> p t h d", h=HG), heads[:, :, :, 0:D],
                                         rc[:].unsqueeze(3).to_broadcast([P, TB, HG, D]), ALU.mult), seen)

        def a_heads_add(n, seen):
            b, g = divmod(n, NG)
            nc.vector.wait_ge(dve, seen[0])
            xs = xt[:, TB * b:TB * b + TB, HG * D * g:HG * D * (g + 1)]
            nc.vector.tensor_tensor(xs, xs, at[:], ALU.add).then_inc(a_x3, 1)

        @block.sync
        def _(sp):
            for b in range(B):
                sp.dma_start(xt[:, TB * b:TB * b + TB, :],
                             x[S * b:S * b + S, :].rearrange("(t p) f -> p t f", p=P)).then_inc(s_x[b], 16)
            for e in range(NE):
                w = W[:, e * WE:(e + 1) * WE]
                for m, src in enumerate((gate[e], up[e])):
                    sp.dma_start(w[:, m * C * I:(m + 1) * C * I].rearrange("p (c n) -> p c n", c=C),
                                 src.rearrange("(c p) n -> p c n", p=P)).then_inc(s_w, 16)
                sp.dma_start(w[:, 2 * C * I:].rearrange("p (i n) -> p i n", i=IC),
                             down[e].rearrange("(i p) n -> p i n", p=P)).then_inc(s_w, 16)
                if e == 2:
                    for b in range(B):
                        write_rows(sp, 0, b)
            sp.wait_ge(s_fin[0], 1)
            rows_written(sp, 0)
            for b in range(B):
                sp.dma_start(xt[:, TB * b:TB * b + TB, :],
                             x2d[S * b:S * b + S, :].rearrange("(t p) f -> p t f", p=P)).then_inc(s_x2[b], 16)
            for b in range(3):
                a_stack(sp, b)
                a_stack_back(sp, b)
            a_max_row(sp, 0)
            for b in range(B):
                if b + 1 < B:
                    a_max_row(sp, b + 1)
                if b + 3 < B:
                    a_stack(sp, b + 3)
                    a_stack_back(sp, b + 3)

        @block.gpsimd
        def _(p):
            seen = [0]
            nc.gpsimd.memset(V[:], 0.0).then_inc(s_const, 1)
            p.wait_ge(s_const, 1)
            nc.gpsimd.memset(V[:, :, :, :, D:D + 1], 1.0).then_inc(s_const, 1)
            p.wait_ge(s_const, 2)
            ln_newton(0, 0, seen)
            ln_newton(0, 1, seen)
            ffn_pool(0)
            nc.gpsimd.memset(area[KROWS:P, :], 0.0).then_inc(s_const, 1)
            p.wait_ge(s_const, 3)
            nc.gpsimd.memset(Ks[KROWS:KROWS + 1], 1.0).then_inc(s_const, 1)
            p.wait_ge(s_const, 4)
            for b in range(5):
                ln_newton(1, b, seen)
            a_mask(0)
            for n in range(NG * B):
                if n + 1 < NG * B:
                    a_mask(n + 1)
                if n % NG == 3:
                    round_newton(n // NG, seen)
            round_newton(B, seen)
            ffn_pool(1)

        @block.scalar
        def _(a):
            for dst, src in ((cf[:], constf), (cb[:], constb),
                             (wr[:], router.rearrange("(c p) e -> p c e", p=P)),
                             (wq_s[:], wq.rearrange("(c p) e -> p c e", p=P)),
                             (wk_s[:], wk.rearrange("(c p) e -> p c e", p=P)),
                             (wv_s[:], wv.rearrange("(c p) e -> p c e", p=P)),
                             (bq_s[:], bq), (bk_s[:], bk), (bv_s[:], bv)):
                a.dma_start(dst, src).then_inc(s_cst, 16)
            for b in range(B):
                if b >= 2:
                    a.wait_ge(s_lp[0], b - 1)
                ln_evacuate(0, b, bank[6 + b % 2])
            route_act(0)
            used = tiles_used(a, 0)
            for j in range(NS + 1):
                ffn_act_step(0, j, j, used)
            for b in range(3):
                ln_evacuate(1, b, bank[6])
                a_split_act(b)
                a_split_act2(b)
                a_split_act3(b)
            ln_evacuate(1, 3, bank[6])
            for u in range(3):
                a_exp(0, u)
            for n in range(NG * B):
                b, g = divmod(n, NG)
                more = n + 1 < NG * B
                prep = b + 3 < B
                if more:
                    a_exp(n + 1, 0)
                if prep and g == 1:
                    a_split_act2(b + 3)
                if prep and g == 2:
                    a_split_act3(b + 3)
                if more:
                    a_exp(n + 1, 1)
                    a_exp(n + 1, 2)
                if g == 2 and b >= 2:
                    ln_evacuate(2, b - 2, bank[6])
                    write_rows(a, 1, b - 2)
                a_values_copy(n)
                if prep and g == 0:
                    a_split_act(b + 3)
                if g == 3 and b + 4 < B:
                    ln_evacuate(1, b + 4, bank[6])
            ln_evacuate(2, B - 2, bank[6])
            write_rows(a, 1, B - 2)
            ln_evacuate(2, B - 1, bank[6])
            write_rows(a, 1, B - 1)
            route_act(1)
            used = tiles_used(a, 1)
            for j in range(NS + 1):
                ffn_act_step(1, j, j, used)

        @block.vector
        def _(v):
            seen = [0]
            ln_stats(0, 0, seen)
            ln_stats(0, 1, seen)
            for b in range(B):
                ln_apply(0, b)
            for b in range(B):
                logits_copy(0, b, bank[4 + b % 2])
            v.wait_ge(s_cst, 16 * 9)
            route_dve(0, seen)
            used = tiles_used(v, 0)
            for j in range(NS + 1):
                ffn_dve_step(0, j, j, used)
            def ln2_stats(b):
                v.wait_ge(s_x2[b], 16)
                ln_stats(1, b, seen)

            ln2_stats(0)
            ln2_stats(1)
            ln2_stats(2)
            v.wait_ge(s_const, 4)
            for b in range(3):
                ln_apply(1, b)
                if b < 2:
                    ln2_stats(b + 3)
                a_split_dve(b)
                a_split_dve2(b)
                a_split_dve3(b)
            ln_apply(1, 3)
            for m in range(NG + 3):
                for u in range(3):
                    a_max_dve(m, u)
                if m == NG - 1:
                    a_neg_dve(0)
                    a_neg_copy(0)
            for n in range(NG * B):
                b, g = divmod(n, NG)
                m = n + NG + 3
                more = m < NG * B
                prep = b + 3 < B
                if g == 1 and prep:
                    a_split_dve(b + 3)
                if n >= 2:
                    a_heads_sum(n - 2, seen)
                if more:
                    a_max_dve(m, 0)
                if n >= 2:
                    a_heads_div(n - 2, seen)
                if g == 1 and b >= 2:
                    ln_apply(2, b - 2)
                if g == 1 and b + 1 < B:
                    a_neg_copy(b + 1)
                if g == 2:
                    round_aggr(b, seen)
                if g == 2:
                    round_eps(b, seen)
                if more:
                    a_max_dve(m, 1)
                if n >= 2:
                    a_heads_add(n - 2, seen)
                if g == 2:
                    round_half(b, seen)
                if g == 1 and prep:
                    a_split_dve2(b + 3)
                if g == 2 and prep:
                    a_split_dve3(b + 3)
                if more:
                    a_max_dve(m, 2)
                if g == 0 and b + 1 < B:
                    a_neg_dve(b + 1)
                if g == 1:
                    round_stats(b, seen)
                if g == 2:
                    round_guess(b, seen)
                if g == 2 and b + 4 < B:
                    ln_apply(1, b + 4)
                if g == 3 and b >= 2:
                    logits_copy(1, b - 2, bank[6])
            for n in (NG * B - 2, NG * B - 1):
                if n == NG * B - 1:
                    ln_apply(2, B - 2)
                a_heads_sum(n, seen)
                a_heads_div(n, seen)
                a_heads_add(n, seen)
            round_stats(B, seen)
            round_aggr(B, seen)
            round_eps(B, seen)
            round_half(B, seen)
            round_guess(B, seen)
            logits_copy(1, B - 2, bank[6])
            ln_apply(2, B - 1)
            logits_copy(1, B - 1, bank[6])
            route_dve(1, seen)
            used = tiles_used(v, 1)
            for j in range(NS + 1):
                ffn_dve_step(1, j, j, used)

        @block.tensor
        def _(pe):
            pe.wait_ge(s_cst, 16 * 9)
            for b in range(B):
                if b >= 2:
                    pe.wait_ge(s_xs[0], b - 1)
                ln_transpose(0, b, bank[6 + b % 2])
                if b >= 1:
                    if b >= 3:
                        pe.wait_ge(s_ls[0], b - 2)
                    logits(0, b - 1, bank[4 + (b - 1) % 2])
            pe.wait_ge(s_ls[0], B - 2)
            logits(0, B - 1, bank[4 + (B - 1) % 2])
            pe.wait_ge(s_ls[0], B)
            route_pe(0)
            pe.wait_ge(s_w, 48 * NE)
            used = tiles_used(pe, 0)
            offs = {0: weights_at(0)}
            for j in range(NS + 1):
                ffn_pe_step(0, j, j, offs, used)
            pe.wait_ge(s_const, 4)
            pe.wait_ge(s_fin[0], 1)
            for b in range(3):
                if b:
                    pe.wait_ge(a_k32, b)
                    pe.wait_ge(a_v, b)
                    pe.wait_ge(a_q32, b)
                ln_transpose(1, b, bank[6])
                a_proj_q(b)
                a_proj_kv(b)
            pe.wait_ge(a_v, 3)
            pe.wait_ge(a_k32, 3)
            ln_transpose(1, 3, bank[6])
            for m in range(NG + 3):
                for u in range(3):
                    a_max_pe(m, u)
                if m == NG - 1:
                    pe.wait_ge(s_xs[1], 4)
                    a_neg_pe(0)
            for u in range(3):
                a_scores(0, u)
            for n in range(NG * B):
                b, g = divmod(n, NG)
                m = n + NG + 3
                if n + 1 < NG * B:
                    a_scores(n + 1, 0)
                if m < NG * B:
                    a_max_pe(m, 0)
                if n + 1 < NG * B:
                    a_scores(n + 1, 1)
                if g == 1:
                    if b >= 3:
                        pe.wait_ge(s_ls[1], b - 2)
                    pe.wait_ge(a_v, min(b + 4, B))
                    pe.wait_ge(a_k32, min(b + 4, B))
                    if b + 1 < B:
                        a_neg_pe(b + 1)
                if g == 2 and b >= 2:
                    pe.wait_ge(a_ms, min(b + 2, B))
                    if b >= 3:
                        pe.wait_ge(s_ls[1], b - 2)
                    ln_transpose(2, b - 2, bank[6])
                if g == 3 and b >= 2:
                    logits(1, b - 2, bank[6])
                if m < NG * B:
                    a_max_pe(m, 1)
                if n + 1 < NG * B:
                    a_scores(n + 1, 2)
                a_values(n)
                if m < NG * B:
                    a_max_pe(m, 2)
                if g == 0 and b + 3 < B:
                    if n >= 2:
                        pe.wait_ge(a_x3, n - 1)
                    a_proj_q(b + 3)
                    a_proj_kv(b + 3)
                if n >= 1:
                    pe.wait_ge(a_q32, min(b + 4, B))
                    a_heads_pe(n - 1)
                if g == 3 and b + 4 < B:
                    pe.wait_ge(a_ms, b + 2)
                    if b >= 2:
                        pe.wait_ge(s_ls[1], b - 1)
                    ln_transpose(1, b + 4, bank[6])
            a_heads_pe(NG * B - 1)
            pe.wait_ge(s_ls[1], B - 2)
            ln_transpose(2, B - 2, bank[6])
            logits(1, B - 2, bank[6])
            pe.wait_ge(s_ls[1], B - 1)
            ln_transpose(2, B - 1, bank[6])
            logits(1, B - 1, bank[6])
            pe.wait_ge(s_ls[1], B)
            route_pe(1)
            used = tiles_used(pe, 1)
            offs = {0: weights_at(0)}
            for j in range(NS + 1):
                ffn_pe_step(1, j, j, offs, used)


def kernel(**inputs):
    import concourse.bacc as bacc
    from concourse.bass_utils import run_bass_kernel_spmd

    a = {k: np.asarray(v) for k, v in inputs.items()}
    cf, cbf = constants()
    import ml_dtypes
    by_head = lambda w: np.ascontiguousarray(w.transpose(1, 0, 2).reshape(H, -1))
    wq = a["L0_attn_Wq"].reshape(NH // 2, 2, H, D).transpose(2, 1, 3, 0).reshape(H, -1)
    bq = a["L0_attn_bq"].reshape(NH // 2, 2, D).transpose(1, 2, 0).reshape(2, P)
    arrays = {
        "x": a["L0_attn_x"].reshape(T, H),
        "wq": np.ascontiguousarray(wq),
        "bq": np.ascontiguousarray(bq.T),
        "wk": np.ascontiguousarray(a["L0_attn_Wk"].transpose(1, 2, 0).reshape(H, -1)),
        "bk": np.ascontiguousarray(a["L0_attn_bk"].T).reshape(NG * D, 1),
        "wv": by_head(a["L0_attn_Wv"]),
        "bv": np.ascontiguousarray(np.broadcast_to(a["L0_attn_bv"].reshape(1, -1), (P, NG * D))),
        "router": a["L0_ffn_router_w"], "gate": a["L0_ffn_gate_w"],
        "up": a["L0_ffn_up_w"], "down": a["L0_ffn_down_w"],
        "constf": cf, "constb": cbf.astype(ml_dtypes.bfloat16),
        "zrow": np.zeros((1, NH * S), ml_dtypes.bfloat16),
    }
    nc = bacc.Bacc("TRN2", target_bir_lowering=False, num_devices=1)
    args = [nc.dram_tensor(n, v.shape, mybir.dt.from_np(v.dtype), kind="ExternalInput").ap()
            for n, v in arrays.items()]
    out = nc.dram_tensor("out", (T, H), F32, kind="ExternalOutput").ap()
    macaron(nc, *args, out)
    r = run_bass_kernel_spmd(nc, [arrays], core_ids=[0])
    return r.results[0]["out"].reshape(B, S, H)
```

```python
from contextlib import ExitStack, nullcontext

import concourse.bass as bass
import numpy as np
from concourse import mybir

F32 = mybir.dt.float32
BF16 = mybir.dt.bfloat16
I32 = mybir.dt.int32
ALU = mybir.AluOpType
ACT = mybir.ActivationFunctionType
AX = mybir.AxisListType

P = 128
B, S, H = 8, 256, 256
T = B * S
NT = T // P
C = H // P
TB = S // P
NE, I = 8, 512
IC = I // P
NS = NT + NE - 1
WE = 3 * C * I
NH, NG, D = 16, 4, 16
HG = NH // NG
PAD = 2 * T
EPS = 1e-5
RSQRT_MAGIC = float(0x5F3759DF)
NEG = -1e30
Q_PART = (0, 0, 0, 2, 1, 1)
K_PART = (2, 1, 0, 0, 0, 1)
KROWS = len(Q_PART) * D
LATE = 9
EARLY = NE // 2
WARM = 10
ROUTE_TILES = (((0, NT),), ((0, NT - TB), (NT - TB, NT)))
SLOT_TILES = ((0, NT // 2), (NT // 2, NT // 2 + 3), (NT // 2 + 3, NT))
XG, OB, QB, VB = 4, 4, 3, 4

CONST = {"ident": P, "desc": NE, "lower": NE * NE, "jrow": NS, "toks": NT * 2}
CONST_AT = dict(zip(CONST, np.cumsum([0] + list(CONST.values())[:-1]).tolist()))
CONST_N = sum(CONST.values())
CONSTB = {"identb": P, "before": P, "ones": P, "iota": P, "mask": HG * P}
CONSTB_AT = dict(zip(CONSTB, np.cumsum([0] + list(CONSTB.values())[:-1]).tolist()))
CONSTB_N = sum(CONSTB.values())


def constants():
    p = np.arange(P)
    f = np.zeros((P, CONST_N), np.float32)
    b = np.zeros((P, CONSTB_N), np.float32)

    def put(a, at, name, v):
        v = np.asarray(v, np.float32).reshape(-1, np.asarray(v).shape[-1])
        a[:, at[name]:at[name] + v.shape[1]] = v

    put(f, CONST_AT, "ident", np.eye(P))
    put(f, CONST_AT, "desc", NE - np.arange(NE)[None])
    put(f, CONST_AT, "lower", (np.arange(NE)[None, :] < np.arange(NE)[:, None]).reshape(1, -1))
    put(f, CONST_AT, "jrow", np.arange(NS)[None])
    toks = np.zeros((P, NT, 2))
    toks[:, :, 0] = P * np.arange(NT)[None] - PAD
    toks[:, :, 1] = p[:, None]
    put(f, CONST_AT, "toks", toks.reshape(P, -1))
    put(b, CONSTB_AT, "identb", np.eye(P))
    put(b, CONSTB_AT, "before", p[:, None] < p[None, :])
    put(b, CONSTB_AT, "ones", np.ones((1, P)))
    put(b, CONSTB_AT, "iota", p[None, :])
    put(b, CONSTB_AT, "mask", np.tile(np.where(p[None, :] > p[:, None], NEG, 0.0), (1, HG)))
    return f, b


def macaron(nc, x, wq, bq, wk, bk, wv, bv, router, gate, up, down, constf, constb, zrow,
            out):
    with ExitStack() as ctx:
        def sb(name, shape, dt=F32):
            return ctx.enter_context(nc.sbuf_tensor(name, shape, dt))

        def sem(name):
            return ctx.enter_context(nc.semaphore(name))

        def dram(name, shape, dt=F32):
            return nc.dram_tensor(name, shape, dt).ap()

        lnrows = dram("lnrows", (T, H))
        rows = dram("rows", (T, 2 * H))
        x2d = dram("x2d", (T, H))
        ffn_out = [x2d, out]

        W = sb("W", [P, NE * WE])
        xt = sb("xt", [P, NT, H])
        xn = sb("xn", [P, 2, TB, H])
        xnT = sb("xnT", [P, 2, C, S])
        xnr = sb("xnr", [P, TB, H])
        xnrT = sb("xnrT", [P, C, S])
        wr = sb("wr", [P, C, NE])
        wq_s = sb("wq_s", [P, C, NH * D])
        wk_s = sb("wk_s", [P, C, NG * D])
        wv_s = sb("wv_s", [P, C, NG * D])
        bq_s = sb("bq_s", [P, 2])
        bk_s = sb("bk_s", [NG * D, 1])
        bv_s = sb("bv_s", [P, NG * D])
        cf = sb("cf", [P, CONST_N])
        cb = sb("cb", [P, CONSTB_N], BF16)
        bn = sb("bn", [P, NT, 6])
        mv = sb("mv", [P, NT, 2])
        ve = sb("ve", [P, NT])
        hv = sb("hv", [P, NT], I32)
        rs = sb("rs", [P, NT], I32)
        nw = sb("nw", [P, NT])
        lg = sb("lg", [P, NT, NE])
        sg = sb("sg", [P, NT, NE])
        mx = sb("mx", [P, NT])
        eq = sb("eq", [P, NT, NE])
        pm = sb("pm", [P, NT])
        oh = sb("oh", [P, NT, NE], BF16)
        tot = sb("tot", [P, NE], I32)
        ntl = sb("ntl", [P, NE], I32)
        lw = sb("lw", [P, NE, NE])
        bt = sb("bt", [P, 3, NE])
        rk = sb("rk", [P, NT, NE])
        pos = sb("pos", [P, NT])
        eg = sb("eg", [1, NS, NE])
        ef = sb("ef", [1, 2, NS])
        eoff = sb("eoff", [1, NS + 1], I32)
        ip = sb("ip", [P, 3, NT], I32)
        jt = sb("jt", [P, NT])
        rb = sb("rb", [P, NT], BF16)
        J = sb("J", [P, NT, NS], BF16)
        vals = sb("vals", [P, NT, 5])
        mh = sb("mh", [P, NT, 2], BF16)
        mr = sb("mr", [P, NT])
        R1 = sb("R1", [P, NT, P], BF16)
        J5 = sb("J5", [P, NT, 5, NS], BF16)
        sl = sb("sl", [P, 5, NS])
        tf = sb("tf", [P, 2, NS])
        sidx = sb("sidx", [P, NS], I32)
        gidx = sb("gidx", [P, NS], I32)
        mp2 = sb("mp2", [P, 2, NS])
        area = sb("area", [P, QB * (NH + NG) * S // 2])
        xn0 = area[:, 0:NT * H].rearrange("p (t f) -> p t f", t=NT)
        lgT = area[0:NE, NT * H:NT * H + T]

        def part(at, *shape):
            n = int(np.prod(shape))
            names = "abc"[:len(shape)]
            v = area[:, at:at + n]
            if len(shape) > 1:
                v = v.rearrange(f"p ({' '.join(names)}) -> p {' '.join(names)}",
                                **dict(zip(names, shape)))
            return v, at + n

        xg, used = part(0, XG, 2 * H)
        xT, used = part(used, 2, C, P)
        sil, used = part(used, 2, I)
        hh, used = part(used, 2, I)
        hT, used = part(used, 2, IC, P)
        ob, area_ffn = part(used, OB, H)
        q32 = sb("q32", [P, 2, S])
        qr = sb("qr", [P, 2, S])
        qp = sb("qp", [P, 2, 3, 2, S], BF16)
        k32 = sb("k32", [NG * D, S])
        kr = sb("kr", [NG * D, S])
        kp = J5[0:NG * D].rearrange("p t k j -> p (t k j)")[:, 0:2 * 3 * S].rearrange(
            "p (r k s) -> p r k s", r=2, k=3)
        half = QB * NH * S // 2
        Qs = area[:, 0:half].bitcast(BF16).rearrange("p (r h s) -> p r h s", r=QB, h=NH)
        Ks = area[:, half:].bitcast(BF16).rearrange("p (r h s) -> p r h s", r=QB, h=NG)
        V = sb("V", [P, VB, TB, NG, 2 * D])
        mxa = sb("mxa", [P, 2, TB, NH])
        nmx = sb("nmx", [P, TB, NH], BF16)
        mT = sb("mT", [NH, S], BF16)
        fin = sb("fin", [1, 2])
        PT = sb("PT", [P, 2, 3 * 512])
        OT = sb("OT", [P, 2, S])
        rc = sb("rc", [P, TB, HG])
        at = sb("at", [P, TB, HG * D])

        bank = [ctx.enter_context(nc.psum_tensor(f"bank{i}", [P, 512], F32)) for i in range(8)]
        bankm = bank[6][:, 0:P].bitcast(BF16)

        def cst(name):
            return cf[:, CONST_AT[name]:CONST_AT[name] + CONST[name]]

        def cstb(name):
            return cb[:, CONSTB_AT[name]:CONSTB_AT[name] + CONSTB[name]]

        ident, identb = cst("ident"), cstb("identb")
        rsf = rs[:].bitcast(F32)

        s_x = [sem(f"s_x{b}") for b in range(B)]
        s_cst = sem("s_cst")
        s_aw = sem("s_aw")
        s_w = [sem(f"s_w{i}") for i in range(NE // EARLY)]
        s_x2 = [sem(f"s_x2_{b}") for b in range(B)]
        s_const = sem("s_const")
        dve = sem("dve")
        pool = sem("pool")
        s_st = [sem(f"s_st{k}") for k in range(3)]
        s_rs = [sem(f"s_rs{k}") for k in range(3)]
        s_xn = [sem(f"s_xn{k}") for k in range(3)]
        s_xp = [sem(f"s_xp{k}") for k in range(3)]
        s_xs = [sem(f"s_xs{k}") for k in range(3)]
        s_row = [sem(f"s_row{l}") for l in range(2)]
        s_pace = sem("s_pace")
        s_lr = sem("s_lr")
        s_lt = sem("s_lt")
        s_lp = [sem(f"s_lp{l}") for l in range(2)]
        s_ls = [sem(f"s_ls{l}") for l in range(2)]
        s_ex = [sem(f"s_ex{l}") for l in range(2)]
        s_oh = [sem(f"s_oh{l}") for l in range(2)]
        s_rk = [sem(f"s_rk{l}") for l in range(2)]
        s_va = [sem(f"s_va{l}") for l in range(2)]
        s_jj = [sem(f"s_jj{l}") for l in range(2)]
        s_r5 = [sem(f"s_r5{l}") for l in range(2)]
        s_rj = [sem(f"s_rj{l}") for l in range(2)]
        s_sl = [sem(f"s_sl{l}") for l in range(2)]
        s_ix = [sem(f"s_ix{l}") for l in range(2)]
        f_g = [[sem(f"f_g{l}_{i}") for i in range(XG)] for l in range(2)]
        f_gx = [sem(f"f_gx{i}") for i in range(XG)]
        f_s = [[sem(f"f_s{l}_{i}") for i in range(OB)] for l in range(2)]
        f_xp = [sem(f"f_xp{l}") for l in range(2)]
        f_xs = [sem(f"f_xs{l}") for l in range(2)]
        f_gp = [sem(f"f_gp{l}") for l in range(2)]
        f_up = [sem(f"f_up{l}") for l in range(2)]
        f_si = [sem(f"f_si{l}") for l in range(2)]
        f_h = [sem(f"f_h{l}") for l in range(2)]
        f_hp = [sem(f"f_hp{l}") for l in range(2)]
        f_hs = [sem(f"f_hs{l}") for l in range(2)]
        f_y = [sem(f"f_y{l}") for l in range(2)]
        f_o = [sem(f"f_o{l}") for l in range(2)]
        a_q = sem("a_q")
        a_kv = sem("a_kv")
        a_q32 = sem("a_q32")
        a_k32 = sem("a_k32")
        a_v = sem("a_v")
        a_qh = sem("a_qh")
        a_qr = sem("a_qr")
        a_qm = sem("a_qm")
        a_ql = sem("a_ql")
        a_qs = [sem(f"a_qs{i}") for i in range(QB)]
        a_a = sem("a_a")
        a_am = sem("a_am")
        a_nm = sem("a_nm")
        a_mp = sem("a_mp")
        a_ms = sem("a_ms")
        a_mq = [sem(f"a_mq{i}") for i in range(QB)]
        a_st = sem("a_st")
        a_e = sem("a_e")
        a_pm = sem("a_pm")
        a_o = sem("a_o")
        a_os = sem("a_os")
        a_ot = sem("a_ot")
        a_x3 = sem("a_x3")
        s_fin = [sem(f"s_fin{l}") for l in range(2)]

        block = ctx.enter_context(nc.Block())

        LN_GROUPS = (((0, 1), (1, 3), (3, 5), (5, B)), ((0, 1), (1, 4), (4, 5)))

        def tiles(k, i):
            b0, b1 = LN_GROUPS[k][i]
            return TB * b0, TB * b1

        def ln_sums(k, t, seen):
            if t % TB == 0:
                nc.vector.wait_ge((s_x, s_x2)[k][t // TB], 16)
            nc.vector.bn_stats(bn[:, t, :], xt[:, t, :]).then_inc(dve, 1)
            seen[0] += 1

        def ln_stats(k, i, seen):
            t0, t1 = tiles(k, i)
            nc.vector.wait_ge(dve, seen[0])
            for t in range(t0, t1):
                nc.vector.bn_aggr(mv[:, t, :], bn[:, t, :]).then_inc(dve, 1)
            seen[0] += t1 - t0
            nc.vector.wait_ge(dve, seen[0])
            link(nc.vector.tensor_scalar(ve[:, t0:t1], mv[:, t0:t1, 1], EPS, None, ALU.add), seen)
            link(nc.vector.tensor_scalar(hv[:, t0:t1], ve[:, t0:t1].bitcast(I32), 1, None,
                                         ALU.arith_shift_right), seen)
            nc.vector.tensor_scalar(rs[:, t0:t1], hv[:, t0:t1], -1.0, RSQRT_MAGIC,
                                    ALU.mult, ALU.add).then_inc(s_st[k], 1)

        def link(ins, seen):
            seen[0] += 1
            ins.then_inc(dve, 1)
            nc.vector.wait_ge(dve, seen[0])

        def mark(ins, seen):
            seen[0] += 1
            ins.then_inc(dve, 1)

        def plink(ins, seen):
            seen[0] += 1
            ins.then_inc(pool, 1)
            nc.gpsimd.wait_ge(pool, seen[0])

        def newton(v, r, n, done, seen):
            for step in range(3):
                plink(nc.gpsimd.tensor_tensor(n, r, r, ALU.mult), seen)
                plink(nc.gpsimd.tensor_tensor(n, n, v, ALU.mult), seen)
                plink(nc.gpsimd.tensor_scalar(n, n, -0.5, 1.5, ALU.mult, ALU.add), seen)
                last = nc.gpsimd.tensor_tensor(r, r, n, ALU.mult)
                if step < 2:
                    plink(last, seen)
            last.then_inc(done, 1)

        def newton_dve(v, r, n, done, seen, beside=()):
            others = iter(beside)

            def then(ins):
                ins.then_inc(dve, 1)
                seen[0] += 1
                written = seen[0]
                other = next(others, None)
                if other:
                    other()
                nc.vector.wait_ge(dve, written)

            for step in range(3):
                then(nc.vector.scalar_tensor_tensor(out=n, in0=r, scalar=-0.5, in1=r,
                                                    op0=ALU.mult, op1=ALU.mult))
                then(nc.vector.tensor_tensor(n, n, v, ALU.mult))
                last = nc.vector.scalar_tensor_tensor(out=r, in0=n, scalar=1.5, in1=r,
                                                      op0=ALU.add, op1=ALU.mult)
                if step < 2:
                    then(last)
            last.then_inc(done, 1)

        def ln_newton(k, i, seen, eng=nc.gpsimd):
            t0, t1 = tiles(k, i)
            v, r, n = ve[:, t0:t1], rsf[:, t0:t1], nw[:, t0:t1]
            eng.wait_ge(s_st[k], i + 1)
            if eng is nc.gpsimd:
                newton(v, r, n, s_rs[k], seen)
                return
            if i == 0:
                beside = [lambda t=t: ln_sums(k, t, seen) for t in range(*tiles(k, 1))]
            else:
                eng.wait_ge(s_rs[k], i)
                beside = [lambda t=t: ln_apply(k, t // TB, eng, (t % TB,)) for t in range(*tiles(k, i - 1))]
            newton_dve(v, r, n, s_rs[k], seen, beside)

        def of_round(a, b):
            a = a.rearrange("p (b t) -> p b t", t=TB)
            lo, hi = max(b - 1, 0), b + 5
            if b == 0:
                return a[:, hi:hi + 1]
            return a[:, lo:hi + 1:hi - lo] if hi < B else a[:, lo:lo + 1]

        def round_tiles(b):
            return ([TB * (b - 1) + i for i in range(TB)] if b >= 1 else []) + \
                   ([TB * (b + 5) + i for i in range(TB)] if b + 5 < B else [])

        def round_stats_next(b, seen):
            nc.vector.wait_ge(s_x2[b + 5], 16)
            for t in range(TB * (b + 5), TB * (b + 6)):
                mark(nc.vector.bn_stats(bn[:, t, :], xt[:, t, :]), seen)

        def round_stats_done(b, seen):
            nc.vector.wait_ge(a_x3, NG * b)
            for t in range(TB * (b - 1), TB * b):
                mark(nc.vector.bn_stats(bn[:, t, :], xt[:, t, :]), seen)

        def round_aggr(b, seen):
            nc.vector.wait_ge(dve, seen[0])
            for t in round_tiles(b):
                mark(nc.vector.bn_aggr(mv[:, t, :], bn[:, t, :]), seen)

        def round_eps(b, seen):
            nc.vector.wait_ge(dve, seen[0])
            mark(nc.vector.tensor_scalar(of_round(ve[:], b), of_round(mv[:, :, 1], b), EPS, None, ALU.add), seen)

        def round_half(b, seen):
            nc.vector.wait_ge(dve, seen[0])
            mark(nc.vector.tensor_scalar(of_round(hv[:], b), of_round(ve[:].bitcast(I32), b), 1, None,
                                         ALU.arith_shift_right), seen)

        def round_guess(b, seen):
            nc.vector.wait_ge(dve, seen[0])
            nc.vector.tensor_scalar(of_round(rs[:], b), of_round(hv[:], b), -1.0, RSQRT_MAGIC,
                                    ALU.mult, ALU.add).then_inc(s_st[2], 1)

        def round_newton(b, seen):
            eng, steps = (nc.vector, newton_dve) if b == B else (nc.gpsimd, newton)
            eng.wait_ge(s_st[2], b + 1)
            steps(of_round(ve[:], b), of_round(rsf, b), of_round(nw[:], b), s_rs[2], seen)

        def ln_apply(k, b, eng=nc.vector, which=range(TB)):
            done, n = ((s_rs[0], 1 + (b >= 1) + (b >= 3) + (b >= 5)), (s_rs[1], 1 + (b >= 1) + (b >= 4)) if b < 5 else (s_rs[2], b - 4),
                       (s_rs[2], b + 2))[k]
            eng.wait_ge(done, n)
            dst = (xn0[:, TB * b:TB * b + TB], xn[:, b % 2], xnr[:])[k]
            if k == 1 and b >= 2:
                eng.wait_ge(s_xp[k], b - 1)
                eng.wait_ge(s_xn[k], TB * b)
            if k == 2 and b >= 1:
                eng.wait_ge(s_row[1], 32 * b)
                eng.wait_ge(s_xp[k], b)
            for i in which:
                t = TB * b + i
                eng.tensor_scalar(dst[:, i, :], xt[:, t, :], mv[:, t, 0:1], rsf[:, t:t + 1],
                                        ALU.subtract, ALU.mult).then_inc(s_xn[k], 1)

        def ln_transpose(k, b, ps):
            src = (xn0[:, TB * b:TB * b + TB], xn[:, b % 2], xnr[:])[k]
            nc.tensor.wait_ge(s_xn[k], TB * (b + 1))
            o = ps[:].rearrange("p (c s) -> p c s", c=C)
            for i in range(TB):
                for c in range(C):
                    last = nc.tensor.transpose(o[:, c, i * P:(i + 1) * P],
                                               src[:, i, c * P:(c + 1) * P], ident)
            last.then_inc(s_xp[k], 1)

        def ln_evacuate(k, b, ps):
            nc.scalar.wait_ge(s_xp[k], b + 1)
            dst = xnT[:, b % 2] if k < 2 else xnrT[:]
            nc.scalar.copy(dst, ps[:].rearrange("p (c s) -> p c s", c=C)).then_inc(s_xs[k], 1)

        def logits(b, ps):
            src = xnrT[:]
            nc.tensor.wait_ge(s_xs[2], b + 1)
            for i in range(TB):
                for c in range(C):
                    last = nc.tensor.matmul(ps[:, i * NE:(i + 1) * NE], src[:, c, i * P:(i + 1) * P],
                                            wr[:, c, :], start=(c == 0), stop=(c == C - 1))
            last.then_inc(s_lp[1], 1)

        def logits_rows(b):
            nc.tensor.wait_ge(s_xs[0], b + 1)
            if b >= 2:
                nc.tensor.wait_ge(s_lt, b - 1)
            for c in range(C):
                last = nc.tensor.matmul(bank[4 + b % 2][0:NE, 0:S], wr[:, c, :], xnT[:, b % 2, c, :],
                                        start=(c == 0), stop=(c == C - 1))
            last.then_inc(s_lr, 1)

        def logits_rows_copy(b):
            nc.scalar.wait_ge(s_lr, b + 1)
            nc.scalar.copy(lgT[:, S * b:S * b + S], bank[4 + b % 2][0:NE, 0:S]).then_inc(s_lt, 1)

        def logits_turn():
            nc.tensor.wait_ge(s_lt, B)
            for t in range(NT):
                last = nc.tensor.transpose(bank[4][:, t * NE:(t + 1) * NE], lgT[:, t * P:(t + 1) * P],
                                           ident[0:NE, 0:NE])
            last.then_inc(s_lp[0], 1)

        def logits_copy(b, ps):
            nc.vector.wait_ge(s_lp[1], b + 1)
            nc.vector.tensor_copy(lg[:, TB * b:TB * b + TB, :],
                                  ps[:, 0:TB * NE].rearrange("p (t e) -> p t e", e=NE)).then_inc(s_ls[1], 1)

        def rows_written(eng, l):
            eng.wait_ge(s_row[l], 16 * (l + 1) * B)

        def write_rows(eng, l, b):
            k = 2 * l
            src = xn0[:, TB * b:TB * b + TB] if k == 0 else xnr[:]
            dst = (lnrows, rows)[l][S * b:S * b + S, :].rearrange("(t p) f -> p t f", p=P)
            eng.wait_ge(s_xn[k], TB * (b + 1))
            if l == 1:
                eng.dma_start(dst[:, :, 0:H], xt[:, TB * b:TB * b + TB, :]).then_inc(s_row[l], 16)
            eng.dma_start(dst[:, :, l * H:l * H + H], src).then_inc(s_row[l], 16)

        def slot_values(eng, t0, t1):
            n = t1 - t0
            return eng.tensor_tensor(J5[:, t0:t1], J[:, t0:t1, :].unsqueeze(2).to_broadcast([P, n, 5, NS]),
                                     vals[:, t0:t1, :].unsqueeze(3).to_broadcast([P, n, 5, NS]), ALU.mult)

        def route_pool(l):
            nc.gpsimd.wait_ge(s_jj[l], 1)
            nc.gpsimd.wait_ge(s_va[l], len(ROUTE_TILES[l]))
            for t0, t1 in SLOT_TILES[:-1]:
                slot_values(nc.gpsimd, t0, t1).then_inc(s_r5[l], 1)

        def route_choice(l, i, seen):
            v = nc.vector
            t0, t1 = ROUTE_TILES[l][i]
            n = t1 - t0
            sgt, mxt, eqt, pmt, mht, mrt = (a[:, t0:t1] for a in (sg, mx, eq, pm, mh, mr))
            v.wait_ge(s_ex[l], i + 1)
            link(v.tensor_scalar(sgt, sgt, 1.0, None, ALU.add), seen)
            link(v.reciprocal(sgt, sgt), seen)
            link(v.tensor_reduce(mxt, sgt, AX.X, ALU.max), seen)
            link(v.tensor_tensor(eqt, sgt, mxt.unsqueeze(2).to_broadcast([P, n, NE]), ALU.is_equal), seen)
            desc = cst("desc").unsqueeze(1).to_broadcast([P, n, NE])
            link(v.tensor_tensor(eqt, eqt, desc, ALU.mult), seen)
            link(v.tensor_reduce(pmt, eqt, AX.X, ALU.max), seen)
            v.tensor_tensor(oh[:, t0:t1], desc, pmt.unsqueeze(2).to_broadcast([P, n, NE]),
                            ALU.is_equal).then_inc(s_oh[l], 1)
            link(v.tensor_copy(mht[:, :, 0], mxt), seen)
            link(v.tensor_tensor(mrt, mxt, mht[:, :, 0], ALU.subtract), seen)
            link(v.tensor_copy(mht[:, :, 1], mrt), seen)
            mark(v.tensor_copy(vals[:, t0:t1, 0:2], cst("toks").rearrange("p (t k) -> p t k", k=2)[:, t0:t1]), seen)
            mark(v.tensor_copy(vals[:, t0:t1, 2:4], mht), seen)
            v.tensor_tensor(vals[:, t0:t1, 4], mrt, mht[:, :, 1], ALU.subtract).then_inc(s_va[l], 1)

        def route_dve(l, seen):
            v = nc.vector
            v.wait_ge(s_rk[l], 1)
            link(v.tensor_scalar(tot[:], bank[4][:, P:P + NE], float(P - 1), None, ALU.add), seen)
            link(v.tensor_scalar(ntl[:], tot[:], P.bit_length() - 1, None, ALU.arith_shift_right), seen)
            link(v.tensor_tensor(lw[:], ntl[:].unsqueeze(1).to_broadcast([P, NE, NE]),
                                 cst("lower").rearrange("p (e f) -> p e f", e=NE), ALU.mult), seen)
            link(v.tensor_reduce(bt[:, 0, :], lw[:], AX.X, ALU.add), seen)
            v.tensor_tensor(bt[:, 1, :], bt[:, 0, :], ntl[:], ALU.add).then_inc(dve, 1)
            seen[0] += 1
            link(v.tensor_scalar(bt[:, 2, :], bt[:, 0, :], float(P), None, ALU.mult), seen)
            link(v.tensor_tensor(rk[:], bank[4][:, 0:P].rearrange("p (t e) -> p t e", e=NE),
                                 bt[:, 2, :].unsqueeze(1).to_broadcast([P, NT, NE]), ALU.add), seen)
            link(v.tensor_tensor(rk[:], rk[:], oh[:], ALU.mult), seen)
            link(v.tensor_reduce(pos[:], rk[:], AX.X, ALU.add), seen)
            link(v.tensor_copy(ip[:, 0, :], pos[:]), seen)
            v.tensor_scalar(ip[:, 1, :], ip[:, 0, :], P.bit_length() - 1, None,
                            ALU.arith_shift_right).then_inc(dve, 1)
            v.tensor_scalar(ip[:, 2, :], ip[:, 0, :], P - 1, None, ALU.bitwise_and).then_inc(dve, 1)
            seen[0] += 2
            v.wait_ge(dve, seen[0])
            v.tensor_copy(jt[:], ip[:, 1, :]).then_inc(dve, 1)
            v.tensor_copy(rb[:], ip[:, 2, :]).then_inc(dve, 1)
            seen[0] += 2
            v.wait_ge(dve, seen[0])
            v.tensor_tensor(J[:], jt[:].unsqueeze(2).to_broadcast([P, NT, NS]),
                            cst("jrow").unsqueeze(1).to_broadcast([P, NT, NS]),
                            ALU.is_equal).then_inc(s_jj[l], 1)
            h = NT // 2
            for t in (0, h):
                v.tensor_tensor(R1[:, t:t + h, :], cstb("iota").unsqueeze(1).to_broadcast([P, h, P]),
                                rb[:, t:t + h].unsqueeze(2).to_broadcast([P, h, P]),
                                ALU.is_equal).then_inc(s_rj[l], 1)
            v.wait_ge(s_jj[l], 1)
            slot_values(v, *SLOT_TILES[-1]).then_inc(s_rj[l], 1)
            link(v.tensor_tensor(eg[:], bt[0:1, 1, :].unsqueeze(1).to_broadcast([1, NS, NE]),
                                 cst("jrow")[0:1, :].unsqueeze(2).to_broadcast([1, NS, NE]), ALU.is_le), seen)
            link(v.tensor_reduce(ef[:, 0, :], eg[:], AX.X, ALU.add), seen)
            v.tensor_scalar(ef[:, 1, :], ef[:, 0, :], float(NE - 1), float(WE), ALU.min, ALU.mult).then_inc(dve, 1)
            seen[0] += 1
            v.wait_ge(dve, seen[0])
            v.tensor_copy(eoff[:, 0:NS], ef[:, 1, :]).then_inc(s_ix[l], 1)
            v.tensor_copy(eoff[:, NS:NS + 1], bt[0:1, 1, NE - 1:NE]).then_inc(s_ix[l], 1)
            v.wait_ge(s_sl[l], 1)
            link(v.tensor_copy(sl[:], bank[5][:, 0:5 * NS].rearrange("p (k j) -> p k j", k=5)), seen)
            link(v.scalar_tensor_tensor(out=tf[:, 0, :], in0=sl[:, 0, :], scalar=float(PAD), in1=sl[:, 1, :],
                                        op0=ALU.add, op1=ALU.add), seen)
            v.tensor_copy(sidx[:], tf[:, 0, :]).then_inc(s_ix[l], 1)
            v.tensor_scalar(gidx[:], tf[:, 0, :], float(T - 1), None, ALU.min).then_inc(s_ix[l], 1)
            link(v.tensor_tensor(mp2[:, 0, :], sl[:, 2, :], sl[:, 3, :], ALU.add), seen)
            link(v.tensor_tensor(mp2[:, 0, :], mp2[:, 0, :], sl[:, 4, :], ALU.add), seen)
            link(v.tensor_scalar(mp2[:, 1, :], mp2[:, 0, :], 0.5, None, ALU.mult), seen)

        def route_act(l, i):
            t0, t1 = ROUTE_TILES[l][i]
            nc.scalar.wait_ge(s_ls[l], t1 // TB)
            nc.scalar.activation(sg[:, t0:t1], lg[:, t0:t1], ACT.Exp, scale=-1.0).then_inc(s_ex[l], 1)

        def warm(n=WARM, ps=bank[3]):
            for i in range(n):
                nc.tensor.matmul(ps[:], identb, cstb("mask"), start=True, stop=True)

        def route_pe(l):
            pe = nc.tensor
            warm()
            pe.wait_ge(s_oh[l], len(ROUTE_TILES[l]))
            o2 = oh[:].rearrange("p t e -> p (t e)")
            pe.matmul(bank[4][:, 0:P], cstb("before"), o2, start=True, stop=False)
            for s in range(1, NT):
                pe.matmul(bank[4][:, s * NE:P], cstb("ones"), o2[:, 0:P - s * NE],
                          start=False, stop=(s == NT - 1))
            for t in range(NT):
                last = pe.matmul(bank[4][:, P:P + NE], cstb("ones"), oh[:, t, :],
                                 start=(t == 0), stop=(t == NT - 1))
            last.then_inc(s_rk[l], 1)
            for t in range(NT):
                if t == 0:
                    pe.wait_ge(s_jj[l], 1)
                    warm(4)
                    pe.wait_ge(s_rj[l], 1)
                    pe.wait_ge(s_r5[l], 1)
                if t == NT // 2:
                    pe.wait_ge(s_rj[l], 3)
                    pe.wait_ge(s_r5[l], 2)
                last = pe.matmul(bank[5][:, 0:5 * NS], R1[:, t, :],
                                 J5[:, t].rearrange("p k j -> p (k j)"), start=(t == 0), stop=(t == NT - 1))
            last.then_inc(s_sl[l], 1)
            pe.wait_ge(s_ix[l], 3)
            warm()

        def tiles_used(eng, l):
            eng.wait_ge(s_ix[l], 4)
            return eng.value_load(eoff[0:1, NS:NS + 1], min_val=NT, max_val=NS)

        def if_tile(eng, used, j):
            return nullcontext() if j < NT else eng.If(used > j)

        def ffn_steps(eng, used, step, last_step):
            for j in range(NS):
                if j > NT - 1:
                    with eng.If(used == j):
                        last_step(j)
                with if_tile(eng, used, j):
                    step(j)
            with eng.If(used == NS):
                last_step(NS)

        def gather_from(table, dst, j, done):
            nc.gpsimd.indirect_dma_start(
                dst, None, table, bass.IndirectOffsetOnAxis(ap=gidx[:, bass.ds(j, 1)], axis=0)).then_inc(done, 16)

        def gather(l, j, k):
            if l == 0:
                gather_from(lnrows, xg[:, k % XG, H:], j, f_g[0][k % XG])
            else:
                gather_from(rows, xg[:, k % XG, :], j, f_g[1][k % XG])

        def gather_x(j, k):
            gather_from(x, xg[:, k % XG, 0:H], j, f_gx[k % XG])

        def scatter(l, j, k):
            nc.gpsimd.indirect_dma_start(
                ffn_out[l], bass.IndirectOffsetOnAxis(ap=sidx[:, bass.ds(j, 1)], axis=0),
                ob[:, k % OB, :], None, bounds_check=T - 1, oob_is_err=False).then_inc(f_s[l][k % OB], 16)

        def scattered(used, l):
            p = nc.gpsimd
            for j in range(NT - OB, NS):
                with if_tile(p, used, j):
                    p.wait_ge(f_s[l][j % OB], 16 * (j // OB + 1))
                    p.nop()
            nc.gpsimd.memset(fin[:], 0.0).then_inc(s_fin[l], 1)

        def ffn_pool(l):
            p = nc.gpsimd
            route_pool(l)
            rows_written(p, l)
            used = tiles_used(p, l)
            for j in range(XG):
                gather(l, j, j)
            if l == 0:
                for j in range(XG):
                    gather_x(j, j)
            for j in range(1, NS + 1):
                with if_tile(p, used, j - 1):
                    p.wait_ge(f_o[l], j)
                    scatter(l, j - 1, j - 1)
                n = j + XG - 1
                if n < NS:
                    with if_tile(p, used, n - 1):
                        gather(l, n, n)
                        if l == 0:
                            gather_x(n, n)
            scattered(used, l)

        def weights_at(j):
            return nc.tensor.value_load(eoff[0:1, bass.ds(j, 1)], min_val=0, max_val=(NE - 1) * WE)

        def other_experts(off):
            with nc.tensor.If(off > (EARLY - 1) * WE):
                nc.tensor.nop().then_inc(s_pace, 2 * EARLY)
                nc.tensor.wait_ge(s_w[1], 48 * EARLY)
                nc.tensor.nop()

        def ffn_transpose(l, n):
            pe = nc.tensor
            pe.wait_ge(f_g[l][n % XG], 16 * (n // XG + 1))
            if n >= 1:
                pe.wait_ge(f_xs[l], n)
            for c in range(C):
                last = pe.transpose(bank[5][:, c * P:(c + 1) * P],
                                    xg[:, n % XG, H + c * P:H + (c + 1) * P], ident)
            last.then_inc(f_xp[l], 1)

        def ffn_transpose_hidden(l, n):
            pe = nc.tensor
            pe.wait_ge(f_h[l], n + 1)
            if n >= 1:
                pe.wait_ge(f_hs[l], n)
            for i in range(IC):
                last = pe.transpose(bank[4][:, i * P:(i + 1) * P], hh[:, n % 2, i * P:(i + 1) * P], ident)
            last.then_inc(f_hp[l], 1)

        def ffn_gate_up(l, j, off):
            pe = nc.tensor
            pe.wait_ge(f_xs[l], j + 1)
            if j >= 2:
                pe.wait_ge(f_si[l], j - 1)
                pe.wait_ge(f_h[l], j - 1)
            for m, done in ((0, f_gp), (1, f_up)):
                for c in range(C):
                    last = pe.matmul(bank[2 * m + j % 2][:], xT[:, j % 2, c, :],
                                     W[:, bass.ds(off + (m * C + c) * I, I)],
                                     start=(c == 0), stop=(c == C - 1))
                last.then_inc(done[l], 1)

        def ffn_down(l, n, off):
            pe = nc.tensor
            pe.wait_ge(f_hs[l], n + 1)
            if n >= 2:
                pe.wait_ge(f_o[l], n - 1)
            for i in range(IC):
                last = pe.matmul(bank[6 + n % 2][:, 0:H], hT[:, n % 2, i, :],
                                 W[:, bass.ds(off + 2 * C * I + i * H, H)],
                                 start=(i == 0), stop=(i == IC - 1))
            last.then_inc(f_y[l], 1)

        def ffn_pe(l):
            pe = nc.tensor
            used = tiles_used(pe, l)
            offs = {0: weights_at(0)}
            if l == 0:
                other_experts(offs[0])

            def step(j):
                if l == 0 and j < LATE:
                    pe.nop().then_inc(s_pace, 1)
                if l == 0 and j == LATE:
                    pe.wait_ge(s_w[1], 48 * EARLY)
                if j == 0:
                    ffn_transpose(l, 0)
                    warm(3)
                else:
                    ffn_transpose_hidden(l, j - 1)
                    if j + 1 < NS:
                        ffn_transpose(l, j + 1)
                ffn_gate_up(l, j, offs[j])
                for n in ([j + 1] if j + 1 < NT else []) + ([j + NS - NT + 1] if NT <= j + NS - NT + 1 < NS
                                                            and j < NT else []):
                    offs[n] = weights_at(n)
                if l == 0 and j + 1 < LATE:
                    other_experts(offs[j + 1])
                if j == 0:
                    ffn_transpose(l, 1)
                else:
                    ffn_down(l, j - 1, offs[j - 1])

            def last_step(j):
                ffn_transpose_hidden(l, j - 1)
                ffn_down(l, j - 1, offs[j - 1])

            ffn_steps(pe, used, step, last_step)

        def ffn_act(l):
            a = nc.scalar

            def copy_hidden(n):
                a.wait_ge(f_hp[l], n + 1)
                if n >= 2:
                    a.wait_ge(f_y[l], n - 1)
                a.copy(hT[:, n % 2], bank[4][:].rearrange("p (i s) -> p i s", i=IC)).then_inc(f_hs[l], 1)

            def step(j):
                if j >= 1:
                    copy_hidden(j - 1)
                a.wait_ge(f_gp[l], j + 1)
                if j >= 2:
                    a.wait_ge(f_h[l], j - 1)
                a.activation(sil[:, j % 2, :], bank[j % 2][:], ACT.Silu).then_inc(f_si[l], 1)

            ffn_steps(a, tiles_used(a, l), step, lambda j: copy_hidden(j - 1))

        def ffn_dve(l):
            v = nc.vector

            def copy_tile(n):
                v.wait_ge(f_xp[l], n + 1)
                if n >= 2:
                    v.wait_ge(f_up[l], n - 1)
                v.tensor_copy(xT[:, n % 2], bank[5][:, 0:H].rearrange("p (c s) -> p c s", c=C)).then_inc(f_xs[l], 1)

            def finish(n):
                v.wait_ge(f_y[l], n + 1)
                if l == 0:
                    v.wait_ge(f_gx[n % XG], 16 * (n // XG + 1))
                if n >= OB:
                    v.wait_ge(f_s[l][n % OB], 16 * (n // OB))
                v.scalar_tensor_tensor(out=ob[:, n % OB, :], in0=bank[6 + n % 2][:, 0:H],
                                       scalar=mp2[:, 1, n:n + 1], in1=xg[:, n % XG, 0:H],
                                       op0=ALU.mult, op1=ALU.add).then_inc(f_o[l], 1)

            def step(j):
                if j == 0:
                    copy_tile(0)
                if j + 1 < NS:
                    copy_tile(j + 1)
                v.wait_ge(f_si[l], j + 1)
                v.wait_ge(f_up[l], j + 1)
                if j >= 2:
                    v.wait_ge(f_hp[l], j - 1)
                v.tensor_tensor(hh[:, j % 2, :], sil[:, j % 2, :], bank[2 + j % 2][:], ALU.mult).then_inc(f_h[l], 1)
                if j >= 1:
                    finish(j - 1)

            ffn_steps(v, tiles_used(v, l), step, lambda j: finish(j - 1))

        def a_proj_q(b, ps=bank[7], halves=(0, 1)):
            pe = nc.tensor
            if 0 in halves:
                pe.wait_ge(s_xs[1], b + 1)
            for m in halves:
                for c in range(C):
                    last = pe.matmul(ps[:, m * S:(m + 1) * S], wq_s[:, c, m * P:(m + 1) * P],
                                     xnT[:, b % 2, c, :], start=(c == 0), stop=(c == C - 1))
            if 1 in halves:
                last.then_inc(a_q, 1)

        def a_proj_k(b, ps=bank[6]):
            for c in range(C):
                nc.tensor.matmul(ps[0:NG * D, 0:S], wk_s[:, c, :], xnT[:, b % 2, c, :],
                                 start=(c == 0), stop=(c == C - 1))

        def a_proj_v(b, ps=bank[6]):
            for i in range(TB):
                for c in range(C):
                    last = nc.tensor.matmul(ps[:, S + i * NG * D:S + (i + 1) * NG * D],
                                            xnT[:, b % 2, c, i * P:(i + 1) * P], wv_s[:, c, :],
                                            start=(c == 0), stop=(c == C - 1))
            last.then_inc(a_kv, 1)

        def a_proj_kv(b, ps=bank[6]):
            a_proj_k(b, ps)
            a_proj_v(b, ps)

        def a_q_bias(b, ps=bank[7]):
            a = nc.scalar
            a.wait_ge(a_q, b + 1)
            if b >= 1:
                a.wait_ge(a_qr, 2 * b)
            for m in range(2):
                last = a.activation(q32[:, m, :], ps[:, m * S:(m + 1) * S], ACT.Identity,
                                    bias=bq_s[:, m:m + 1])
            last.then_inc(a_q32, 1)

        def a_leading(b):
            a = nc.scalar
            if b >= 2:
                a.wait_ge(a_qs[(b - 2) % QB], stacks_written(b - 2))
            a.wait_ge(a_q32, b + 1)
            a.copy(qp[:, b % 2, 0], q32[:]).then_inc(a_qh, 1)
            a.wait_ge(a_k32, b + 1)
            a.copy(kp[:, b % 2, 0], k32[:]).then_inc(a_qh, 1)

        def a_middle(b):
            a = nc.scalar
            a.wait_ge(a_qr, 2 * b + 1)
            a.copy(qp[:, b % 2, 1], qr[:]).then_inc(a_qm, 1)
            a.wait_ge(a_qr, 2 * b + 2)
            a.copy(kp[:, b % 2, 1], kr[:]).then_inc(a_qm, 1)

        def a_kv_bias(b, ps=bank[6]):
            v = nc.vector
            v.wait_ge(a_kv, b + 1)
            if b >= 1:
                v.wait_ge(a_qr, 2 * b)
            v.tensor_scalar(k32[:], ps[0:NG * D, 0:S], bk_s[:], None, ALU.add).then_inc(a_k32, 1)
            v.tensor_tensor(V[:, b % VB, :, :, 0:D],
                            ps[:, S:S + TB * NG * D].rearrange("p (t g d) -> p t g d", t=TB, g=NG),
                            bv_s[:].rearrange("p (g d) -> p g d", g=NG).unsqueeze(1).to_broadcast([P, TB, NG, D]),
                            ALU.add).then_inc(a_v, 1)

        def a_left(b, v=nc.vector):
            v.wait_ge(a_qh, 2 * b + 1)
            if b >= 1:
                v.wait_ge(a_ql, 2 * b)
            v.tensor_tensor(qr[:], q32[:], qp[:, b % 2, 0], ALU.subtract).then_inc(a_qr, 1)
            v.wait_ge(a_qh, 2 * b + 2)
            v.tensor_tensor(kr[:], k32[:], kp[:, b % 2, 0], ALU.subtract).then_inc(a_qr, 1)

        def a_last(b, v=nc.vector):
            v.wait_ge(a_qm, 2 * b + 1)
            v.tensor_tensor(qp[:, b % 2, 2], qr[:], qp[:, b % 2, 1], ALU.subtract).then_inc(a_ql, 1)
            v.wait_ge(a_qm, 2 * b + 2)
            v.tensor_tensor(kp[:, b % 2, 2], kr[:], kp[:, b % 2, 1], ALU.subtract).then_inc(a_ql, 1)

        def a_stack(sp, b, parts=range(3)):
            r = b % QB
            if b >= QB and 0 in parts:
                sp.wait_ge(a_st, 3 * NG * (b - QB + 1))
                sp.dma_start(Qs[KROWS:KROWS + 1, r], zrow.rearrange("o (h s) -> o h s", h=NH)).then_inc(a_qs[r], 16)
            for part in parts:
                ready = (a_qh, a_qm, a_ql)[part]
                sp.wait_ge(ready, 2 * b + 1)
                third = qp[:, b % 2, part].rearrange("p m s -> p (m s)")
                for k in [k for k, q in enumerate(Q_PART) if q == part]:
                    sp.dma_start(Qs[k * D:k * D + D, r].rearrange("d h s -> d (h s)"),
                                 third).then_inc(a_qs[r], 16)
                sp.wait_ge(ready, 2 * b + 2)
                third = kp[:, b % 2, part]
                for k in [k for k, q in enumerate(K_PART) if q == part]:
                    sp.dma_start(Ks[k * D:k * D + D, r].rearrange("d g s -> d (g s)"), third).then_inc(a_qs[r], 16)

        def stacks_written(b):
            use = b // QB
            return 16 * (len(Q_PART) + len(K_PART)) * (use + 1) + 16 * use

        def a_max_row(sp, b):
            r = b % QB
            sp.wait_ge(a_ms, b + 1)
            sp.dma_start(Qs[KROWS:KROWS + 1, r].rearrange("o h s -> o (h s)"), mT[:]).then_inc(a_mq[r], 16)

        def a_max_pe(m, u):
            pe = nc.tensor
            b, g = divmod(m, NG)
            r = b % QB
            if g == 0 and u == 0:
                pe.wait_ge(a_qs[r], stacks_written(b))
            n = 3 * m + u
            if n >= 2:
                pe.wait_ge(a_am, n - 1)
            o = bank[3 + n % 2]
            if u == 0:
                for h in range(HG):
                    pe.matmul(o[:, h * P:(h + 1) * P], Qs[:, r, HG * g + h, 0:P],
                              Ks[:, r, g, 0:P], start=(h == 0), stop=False)
                last = pe.matmul(o[:], identb, cstb("mask"), start=False, stop=True)
            else:
                for h in range(2):
                    pe.matmul(o[:, h * S:(h + 1) * S], Qs[:, r, HG * g + 2 * (u - 1) + h, P:S],
                              Ks[:, r, g, :], start=(h == 0), stop=False)
                last = pe.matmul(o[:].rearrange("p (h k) -> p h k", h=2)[:, :, P:S], identb,
                                 cstb("mask")[:, 0:2 * P].rearrange("p (h k) -> p h k", h=2),
                                 start=False, stop=True)
            last.then_inc(a_a, 1)

        def a_max_dve(m, u):
            v = nc.vector
            b, g = divmod(m, NG)
            n = 3 * m + u
            v.wait_ge(a_a, n + 1)
            o = bank[3 + n % 2]
            if u == 0:
                v.tensor_reduce(mxa[:, b % 2, 0, HG * g:HG * g + HG],
                                o[:].rearrange("p (h k) -> p h k", h=HG), AX.X, ALU.max).then_inc(a_am, 1)
            else:
                h0 = HG * g + 2 * (u - 1)
                v.tensor_reduce(mxa[:, b % 2, 1, h0:h0 + 2],
                                o[:].rearrange("p (h k) -> p h k", h=2), AX.X, ALU.max).then_inc(a_am, 1)

        def a_neg_dve(b):
            v = nc.vector
            v.wait_ge(a_am, 3 * NG * (b + 1))
            if b >= 1:
                v.wait_ge(a_mp, b)
            v.tensor_scalar(nmx[:], mxa[:, b % 2], -1.0, None, ALU.mult).then_inc(a_nm, 1)

        def a_neg_pe(b):
            pe = nc.tensor
            pe.wait_ge(a_nm, b + 1)
            for i in range(TB):
                last = pe.transpose(bankm[0:NH, i * P:(i + 1) * P], nmx[:, i, :], identb)
            last.then_inc(a_mp, 1)

        def a_neg_copy(b):
            v = nc.vector
            v.wait_ge(a_mp, b + 1)
            if b >= 1:
                v.wait_ge(a_mq[(b - 1) % QB], 16 * ((b - 1) // QB + 1))
            v.tensor_copy(mT[:], bankm[0:NH, 0:S]).then_inc(a_ms, 1)

        def a_scores(n, u):
            pe = nc.tensor
            b, g = divmod(n, NG)
            r = b % QB
            if g == 0 and u == 0:
                pe.wait_ge(a_mq[r], 16 * (b // QB + 1))
            if n >= 1:
                pe.wait_ge(a_e, 3 * (n - 1) + u + 1)
            if u < 2:
                rhs = Qs[:, r, HG * g + 2 * u:HG * g + 2 * u + 2, :]
                o = bank[u][:].rearrange("p (h q) -> p h q", h=2)
                k0 = 0
            else:
                rhs = Qs[:, r, HG * g:HG * g + HG, P:S]
                o = bank[u][:].rearrange("p (h q) -> p h q", h=HG)
                k0 = P
            pe.matmul(o, Ks[:, r, g, k0:k0 + P], rhs, start=True, stop=True).then_inc(a_st, 1)

        def a_exp(n, u):
            a = nc.scalar
            a.wait_ge(a_st, 3 * n + u + 1)
            if u == 0 and n >= 2:
                a.wait_ge(a_o, n - 1)
            a.activation(PT[:, n % 2, u * 512:(u + 1) * 512], bank[u][:], ACT.Exp,
                         scale=D ** -0.5).then_inc(a_e, 1)

        def a_mask(n):
            p = nc.gpsimd
            for u, src in ((2, PT[:, n % 2, 0:1024].rearrange("p (h q) -> p h q", h=HG)[:, :, 0:P]),
                           (3, PT[:, n % 2, 1024:1536].rearrange("p (h q) -> p h q", h=HG))):
                p.wait_ge(a_e, 3 * n + u)
                p.affine_select(out=src, in_=src, compare_op=ALU.is_ge, fill=0.0, base=0,
                                pattern=[[0, HG], [1, P]], channel_multiplier=-1).then_inc(a_pm, 1)

        def a_values(n):
            pe = nc.tensor
            b, g = divmod(n, NG)
            pe.wait_ge(a_pm, 2 * n + 2)
            pe.wait_ge(a_v, b + 1)
            if n >= 1:
                pe.wait_ge(a_os, n)
            c0 = (n % 2) * S
            for h in range(HG):
                pe.matmul(bank[5][32 * h:32 * h + 32, c0:c0 + S], V[:, b % VB, 0, g, :],
                          PT[:, n % 2, h * S:(h + 1) * S], start=True, stop=False, tile_position=(0, 32 * h))
            for h in range(HG):
                last = pe.matmul(bank[5][32 * h:32 * h + 32, c0 + P:c0 + S], V[:, b % VB, 1, g, :],
                                 PT[:, n % 2, 1024 + h * P:1024 + (h + 1) * P], start=False, stop=True,
                                 tile_position=(0, 32 * h))
            last.then_inc(a_o, 1)

        def a_values_copy(n):
            a = nc.scalar
            a.wait_ge(a_o, n + 1)
            if n >= 2:
                a.wait_ge(a_ot, n - 1)
            a.copy(OT[:, n % 2, :], bank[5][:, (n % 2) * S:(n % 2) * S + S]).then_inc(a_os, 1)

        def a_heads_pe(n):
            pe = nc.tensor
            pe.wait_ge(a_os, n + 1)
            if n >= 1:
                pe.wait_ge(a_x3, n)
            for i in range(TB):
                last = pe.transpose(bank[7][:, i * P:(i + 1) * P], OT[:, n % 2, i * P:(i + 1) * P], ident)
            last.then_inc(a_ot, 1)

        heads = bank[7][:, 0:S].rearrange("p (t h d) -> p t h d", t=TB, h=HG)

        def a_heads_sum(n, seen):
            nc.vector.wait_ge(a_ot, n + 1)
            mark(nc.vector.reciprocal(rc[:], heads[:, :, :, D]), seen)

        def a_heads_div(n, seen):
            nc.vector.wait_ge(dve, seen[0])
            mark(nc.vector.tensor_tensor(at[:].rearrange("p t (h d) -> p t h d", h=HG), heads[:, :, :, 0:D],
                                         rc[:].unsqueeze(3).to_broadcast([P, TB, HG, D]), ALU.mult), seen)

        def a_heads_add(n, seen):
            b, g = divmod(n, NG)
            nc.vector.wait_ge(dve, seen[0])
            xs = xt[:, TB * b:TB * b + TB, HG * D * g:HG * D * (g + 1)]
            nc.vector.tensor_tensor(xs, xs, at[:], ALU.add).then_inc(a_x3, 1)

        PRO_T = (bank[6], bank[0], bank[6], bank[6])
        PRO_Q = (bank[7], bank[1], bank[7])
        PRO_KV = (bank[5], bank[2], bank[5])

        @block.sync
        def _(sp):
            for b in range(B):
                sp.dma_start(xt[:, TB * b:TB * b + TB, :],
                             x[S * b:S * b + S, :].rearrange("(t p) f -> p t f", p=P)).then_inc(s_x[b], 16)
            def load_expert(e):
                w = W[:, e * WE:(e + 1) * WE]
                for m, src in enumerate((gate[e], up[e])):
                    sp.dma_start(w[:, m * C * I:(m + 1) * C * I].rearrange("p (c n) -> p c n", c=C),
                                 src.rearrange("(c p) n -> p c n", p=P)).then_inc(s_w[e // EARLY], 16)
                sp.dma_start(w[:, 2 * C * I:].rearrange("p (i n) -> p i n", i=IC),
                             down[e].rearrange("(i p) n -> p i n", p=P)).then_inc(s_w[e // EARLY], 16)

            load_expert(0)
            for b in range(B):
                write_rows(sp, 0, b)
            for e in range(1, EARLY):
                load_expert(e)
            for e in range(EARLY, NE):
                sp.wait_ge(s_pace, 2 * (e - EARLY) + 1)
                load_expert(e)
            for dst, src in ((wq_s[:], wq.rearrange("(c p) e -> p c e", p=P)),
                             (wk_s[:], wk.rearrange("(c p) e -> p c e", p=P)),
                             (wv_s[:], wv.rearrange("(c p) e -> p c e", p=P)),
                             (bq_s[:], bq), (bk_s[:], bk), (bv_s[:], bv)):
                sp.dma_start(dst, src).then_inc(s_aw, 16)
            sp.wait_ge(s_fin[0], 1)
            rows_written(sp, 0)
            for b in range(B):
                sp.dma_start(xt[:, TB * b:TB * b + TB, :],
                             x2d[S * b:S * b + S, :].rearrange("(t p) f -> p t f", p=P)).then_inc(s_x2[b], 16)
            a_stack(sp, 0)
            a_stack(sp, 1)
            a_stack(sp, 2, (0, 1))
            a_max_row(sp, 0)
            a_stack(sp, 2, (2,))
            for b in range(B):
                if b + 1 < B:
                    a_max_row(sp, b + 1)
                if b + 3 < B:
                    a_stack(sp, b + 3)

        @block.gpsimd
        def _(p):
            seen = [0]
            nc.gpsimd.memset(V[:], 0.0).then_inc(s_const, 1)
            p.wait_ge(s_const, 1)
            nc.gpsimd.memset(V[:, :, :, :, D:D + 1], 1.0).then_inc(s_const, 1)
            p.wait_ge(s_const, 2)
            for i in range(1, len(LN_GROUPS[0]) - 1):
                ln_newton(0, i, seen)
            p.wait_ge(s_rs[0], len(LN_GROUPS[0]) - 1)
            nc.gpsimd.memset(area[KROWS:P, area_ffn:], 0.0).then_inc(s_const, 1)
            p.wait_ge(s_const, 3)
            nc.gpsimd.memset(Ks[KROWS:KROWS + 1], 1.0).then_inc(s_const, 1)
            p.wait_ge(s_const, 4)
            ffn_pool(0)
            nc.gpsimd.memset(area[KROWS:P, 0:area_ffn], 0.0).then_inc(s_const, 1)
            p.wait_ge(s_const, 5)
            ln_newton(1, 1, seen)
            ln_apply(1, 2, p)
            a_left(1, p)
            a_last(1, p)
            a_left(2, p)
            a_last(2, p)
            ln_newton(1, 2, seen)
            a_mask(0)
            for n in range(NG * B):
                if n + 1 < NG * B:
                    a_mask(n + 1)
                b, g = divmod(n, NG)
                if g < TB and b + 4 < B:
                    ln_apply(1, b + 4, p, (g,))
                if g == 2 and b + 3 < B:
                    a_last(b + 3, p)
                if g == 3:
                    round_newton(b, seen)
            ffn_pool(1)

        @block.scalar
        def _(a):
            for dst, src in ((cf[:], constf), (wr[:], router.rearrange("(c p) e -> p c e", p=P)),
                             (cb[:], constb)):
                a.dma_start(dst, src).then_inc(s_cst, 16)
            for b in range(B):
                if b >= 2:
                    a.wait_ge(s_lr, b - 1)
                ln_evacuate(0, b, bank[6 + b % 2])
                if b >= 1:
                    logits_rows_copy(b - 1)
            logits_rows_copy(B - 1)
            route_act(0, 0)
            ffn_act(0)
            for b in range(3):
                ln_evacuate(1, b, PRO_T[b])
                a_q_bias(b, PRO_Q[b])
                a_leading(b)
                a_middle(b)
            ln_evacuate(1, 3, PRO_T[3])
            for u in range(3):
                a_exp(0, u)
            for n in range(NG * B):
                b, g = divmod(n, NG)
                more = n + 1 < NG * B
                prep = b + 3 < B
                if more:
                    a_exp(n + 1, 0)
                if prep and g == 1:
                    a_leading(b + 3)
                if prep and g == 2:
                    a_middle(b + 3)
                if more:
                    a_exp(n + 1, 1)
                    a_exp(n + 1, 2)
                if g == 2 and b >= 2:
                    ln_evacuate(2, b - 2, bank[6])
                    write_rows(a, 1, b - 2)
                a_values_copy(n)
                if prep and g == 0:
                    a_q_bias(b + 3)
                if g == 3 and b + 4 < B:
                    ln_evacuate(1, b + 4, bank[6])
            ln_evacuate(2, B - 2, bank[6])
            write_rows(a, 1, B - 2)
            route_act(1, 0)
            ln_evacuate(2, B - 1, bank[6])
            write_rows(a, 1, B - 1)
            route_act(1, 1)
            ffn_act(1)

        @block.vector
        def _(v):
            seen = [0]
            for t in range(*tiles(0, 0)):
                ln_sums(0, t, seen)
            ln_stats(0, 0, seen)
            ln_newton(0, 0, seen, v)
            for i in range(1, len(LN_GROUPS[0]) + 1):
                if i < len(LN_GROUPS[0]):
                    ln_stats(0, i, seen)
                if i == len(LN_GROUPS[0]) - 1:
                    ln_newton(0, i, seen, v)
                else:
                    for b in range(*LN_GROUPS[0][i - 1]):
                        ln_apply(0, b)
                if i + 1 < len(LN_GROUPS[0]):
                    for t in range(*tiles(0, i + 1)):
                        ln_sums(0, t, seen)
            v.wait_ge(s_lp[0], 1)
            v.tensor_copy(lg[:], bank[4][:, 0:NT * NE].rearrange("p (t e) -> p t e", e=NE)).then_inc(s_ls[0], B)
            v.wait_ge(s_cst, 16 * 3)
            route_choice(0, 0, seen)
            route_dve(0, seen)
            ffn_dve(0)
            for t in range(*tiles(1, 0)):
                ln_sums(1, t, seen)
            ln_stats(1, 0, seen)
            ln_newton(1, 0, seen, v)
            ln_apply(1, 0)
            ln_stats(1, 1, seen)
            v.wait_ge(s_const, 4)
            for t in range(*tiles(1, 2)):
                ln_sums(1, t, seen)
            ln_apply(1, 1)
            a_kv_bias(0, PRO_KV[0])
            a_left(0)
            a_last(0)
            ln_stats(1, 2, seen)
            a_kv_bias(1, PRO_KV[1])
            for m in range(NG + 3):
                for u in range(3):
                    a_max_dve(m, u)
                if m == 1:
                    ln_apply(1, 3)
                if m == 2:
                    a_kv_bias(2, PRO_KV[2])
                if m == 3:
                    a_neg_dve(0)
                    a_neg_copy(0)
            for n in range(NG * B):
                b, g = divmod(n, NG)
                m = n + NG + 3
                more = m < NG * B
                prep = b + 3 < B
                if g == 1 and prep:
                    a_kv_bias(b + 3)
                if n >= 2:
                    a_heads_sum(n - 2, seen)
                if more:
                    a_max_dve(m, 0)
                if n >= 2:
                    a_heads_div(n - 2, seen)
                if g == 2 and b >= 1:
                    round_stats_done(b, seen)
                if g == 1 and b + 1 < B:
                    a_neg_copy(b + 1)
                if g == 3 and b >= 2:
                    logits_copy(b - 2, bank[6])
                if n >= 2:
                    a_heads_add(n - 2, seen)
                if more:
                    a_max_dve(m, 1)
                if g == 2:
                    round_aggr(b, seen)
                if g == 1 and prep:
                    a_left(b + 3)
                if g == 2:
                    round_eps(b, seen)
                if more:
                    a_max_dve(m, 2)
                if g == 2:
                    round_half(b, seen)
                if g == 0 and b + 1 < B:
                    a_neg_dve(b + 1)
                if g == 0 and b + 5 < B:
                    round_stats_next(b, seen)
                if g == 0 and b >= 2:
                    ln_apply(2, b - 2)
                if g == 2:
                    round_guess(b, seen)
            for n in (NG * B - 2, NG * B - 1):
                if n == NG * B - 1:
                    ln_apply(2, B - 2)
                a_heads_sum(n, seen)
                a_heads_div(n, seen)
                a_heads_add(n, seen)
            round_stats_done(B, seen)
            round_aggr(B, seen)
            round_eps(B, seen)
            round_half(B, seen)
            round_guess(B, seen)
            round_newton(B, seen)
            logits_copy(B - 2, bank[6])
            ln_apply(2, B - 1)
            route_choice(1, 0, seen)
            logits_copy(B - 1, bank[6])
            route_choice(1, 1, seen)
            route_dve(1, seen)
            ffn_dve(1)

        @block.tensor
        def _(pe):
            pe.wait_ge(s_cst, 16 * 3)
            pe.wait_ge(s_st[0], 1)
            warm()
            for b in range(B):
                if b >= 2:
                    pe.wait_ge(s_xs[0], b - 1)
                ln_transpose(0, b, bank[6 + b % 2])
                if b >= 1:
                    logits_rows(b - 1)
            logits_rows(B - 1)
            logits_turn()
            pe.wait_ge(s_ls[0], B)
            route_pe(0)
            pe.wait_ge(s_w[0], 48 * EARLY)
            ffn_pe(0)
            pe.wait_ge(s_aw, 16 * 6)
            pe.wait_ge(s_fin[0], 1)
            pe.wait_ge(s_st[1], 1)
            warm()
            for b in range(2):
                ln_transpose(1, b, PRO_T[b])
                a_proj_q(b, PRO_Q[b])
                a_proj_kv(b, PRO_KV[b])
            pe.wait_ge(s_const, 5)
            for m in range(NG + 3):
                for u in range(3):
                    a_max_pe(m, u)
                    if 2 <= m <= NG + 1:
                        warm(1, bank[0])
                    if (m, u) == (0, 1):
                        ln_transpose(1, 2, PRO_T[2])
                    if (m, u) == (0, 2):
                        pe.wait_ge(a_q32, 1)
                        pe.wait_ge(a_v, 1)
                        pe.wait_ge(a_k32, 1)
                        a_proj_q(2, PRO_Q[2], (0,))
                    if (m, u) == (1, 0):
                        a_proj_q(2, PRO_Q[2], (1,))
                    if (m, u) == (1, 1):
                        a_proj_k(2, PRO_KV[2])
                    if (m, u) == (1, 2):
                        a_proj_v(2, PRO_KV[2])
                    if (m, u) == (2, 1):
                        pe.wait_ge(s_xs[1], 3)
                        ln_transpose(1, 3, PRO_T[3])
                if m == NG - 1:
                    pe.wait_ge(s_xs[1], 4)
                    a_neg_pe(0)
                if m == NG + 1:
                    for u in range(3):
                        a_scores(0, u)
            for n in range(NG * B):
                b, g = divmod(n, NG)
                m = n + NG + 3
                if n + 1 < NG * B:
                    a_scores(n + 1, 0)
                if m < NG * B:
                    a_max_pe(m, 0)
                if n + 1 < NG * B:
                    a_scores(n + 1, 1)
                if g == 1:
                    if b >= 3:
                        pe.wait_ge(s_ls[1], b - 2)
                    pe.wait_ge(a_v, min(b + 4, B))
                    pe.wait_ge(a_k32, min(b + 4, B))
                    if b + 1 < B:
                        a_neg_pe(b + 1)
                if g == 2 and b >= 2:
                    pe.wait_ge(a_ms, min(b + 2, B))
                    if b >= 3:
                        pe.wait_ge(s_ls[1], b - 2)
                    ln_transpose(2, b - 2, bank[6])
                if g == 3 and b >= 2:
                    logits(b - 2, bank[6])
                if m < NG * B:
                    a_max_pe(m, 1)
                if n + 1 < NG * B:
                    a_scores(n + 1, 2)
                a_values(n)
                if m < NG * B:
                    a_max_pe(m, 2)
                if g == 0 and b + 3 < B:
                    if n >= 2:
                        pe.wait_ge(a_x3, n - 1)
                    a_proj_q(b + 3)
                    a_proj_kv(b + 3)
                if g == 0 and b == B - 3:
                    pe.wait_ge(s_ls[1], b - 2)
                    warm(5, bank[6])
                if n >= 1:
                    pe.wait_ge(a_q32, min(b + 4, B))
                    a_heads_pe(n - 1)
                if g == 3 and b + 4 < B:
                    pe.wait_ge(a_ms, b + 2)
                    if b >= 2:
                        pe.wait_ge(s_ls[1], b - 1)
                    ln_transpose(1, b + 4, bank[6])
            a_heads_pe(NG * B - 1)
            pe.wait_ge(s_ls[1], B - 2)
            ln_transpose(2, B - 2, bank[6])
            logits(B - 2, bank[6])
            pe.wait_ge(s_ls[1], B - 1)
            ln_transpose(2, B - 1, bank[6])
            logits(B - 1, bank[6])
            pe.wait_ge(s_ls[1], B)
            route_pe(1)
            ffn_pe(1)


def kernel(**inputs):
    import concourse.bacc as bacc
    from concourse.bass_utils import run_bass_kernel_spmd

    a = {k: np.asarray(v) for k, v in inputs.items()}
    cf, cbf = constants()
    import ml_dtypes
    by_head = lambda w: np.ascontiguousarray(w.transpose(1, 0, 2).reshape(H, -1))
    wq = a["L0_attn_Wq"].reshape(NH // 2, 2, H, D).transpose(2, 1, 3, 0).reshape(H, -1)
    bq = a["L0_attn_bq"].reshape(NH // 2, 2, D).transpose(1, 2, 0).reshape(2, P)
    arrays = {
        "x": a["L0_attn_x"].reshape(T, H),
        "wq": np.ascontiguousarray(wq),
        "bq": np.ascontiguousarray(bq.T),
        "wk": np.ascontiguousarray(a["L0_attn_Wk"].transpose(1, 2, 0).reshape(H, -1)),
        "bk": np.ascontiguousarray(a["L0_attn_bk"].T).reshape(NG * D, 1),
        "wv": by_head(a["L0_attn_Wv"]),
        "bv": np.ascontiguousarray(np.broadcast_to(a["L0_attn_bv"].reshape(1, -1), (P, NG * D))),
        "router": a["L0_ffn_router_w"], "gate": a["L0_ffn_gate_w"],
        "up": a["L0_ffn_up_w"], "down": a["L0_ffn_down_w"],
        "constf": cf, "constb": cbf.astype(ml_dtypes.bfloat16),
        "zrow": np.zeros((1, NH * S), ml_dtypes.bfloat16),
    }
    nc = bacc.Bacc("TRN2", target_bir_lowering=False, num_devices=1)
    args = [nc.dram_tensor(n, v.shape, mybir.dt.from_np(v.dtype), kind="ExternalInput").ap()
            for n, v in arrays.items()]
    out = nc.dram_tensor("out", (T, H), F32, kind="ExternalOutput").ap()
    macaron(nc, *args, out)
    r = run_bass_kernel_spmd(nc, [arrays], core_ids=[0])
    return r.results[0]["out"].reshape(B, S, H)
```
